# Optimizing a Trainium2 kernel written in Bass

```python
import numpy as np
import jax
import jax.numpy as jnp

def _softmax(x, axis=-1):
    return jax.nn.softmax(x, axis=axis)

def _gelu(x):
    return jax.nn.gelu(x, approximate=True)

def _silu(x):
    return jax.nn.silu(x)

def _sigmoid(x):
    return jax.nn.sigmoid(x)

def _layernorm(x, axis=-1, eps=1e-05):
    m = jnp.mean(x, axis=axis, keepdims=True)
    v = jnp.var(x, axis=axis, keepdims=True)
    return (x - m) / jnp.sqrt(v + eps)

def _scatter_add(tgt, idx, src, axis=0):
    return tgt.at[idx].add(src)

def _segment_sum(src, seg, n):
    return jax.ops.segment_sum(src, seg, n)
kernel_name = 'mk_seq_preln_d1_jaxref_r4_1eb070'

def setup_inputs(seed: int=0):
    np.random.seed(seed)
    _w = jnp.asarray

    def _L0_attn_setup():
        import jax, jax.numpy as jnp
        import numpy as np
        import math
        B, N, E, D = (4, 2048, 256, 64)
        key = jax.random.key(seed)
        kx, kq, kk, kv, ko = jax.random.split(key, 5)
        x = jax.random.normal(kx, (B, N, E), dtype=jnp.float32)
        wq = jnp.sign(jax.random.normal(kq, (D, E), dtype=jnp.float32)) / math.sqrt(E)
        wk = jnp.sign(jax.random.normal(kk, (D, E), dtype=jnp.float32)) / math.sqrt(E)
        wv = jnp.sign(jax.random.normal(kv, (D, E), dtype=jnp.float32)) / math.sqrt(E)
        wo = jnp.sign(jax.random.normal(ko, (E, D), dtype=jnp.float32)) / math.sqrt(D)
        return {'x': x, 'wq': wq, 'wk': wk, 'wv': wv, 'wo': wo}
    _L0_attn_in = _L0_attn_setup()

    def _L0_ffn_setup():
        import jax, jax.numpy as jnp
        import numpy as np
        from jax import lax
        H = 256
        E = 8
        E_MLP = E - 4
        TOP_K = 2
        I = 128
        KC = 4
        SHARED_SCALE = 1.0
        key = jax.random.key(seed)
        ks = jax.random.split(key, 8)
        B, S = (4, 1024)
        s_h = 1.0 / np.sqrt(H)
        s_i = 1.0 / np.sqrt(I)
        return {'hidden_states': jax.random.normal(ks[0], (B, S, H), dtype=jnp.float32), 'Wr': jax.random.normal(ks[1], (H, E), dtype=jnp.float32) * s_h, 'router_bias': jnp.zeros((E,), dtype=jnp.float32), 'Wg': jax.random.normal(ks[2], (E_MLP, H, I), dtype=jnp.float32) * s_h, 'Wu': jax.random.normal(ks[3], (E_MLP, H, I), dtype=jnp.float32) * s_h, 'Wd': jax.random.normal(ks[4], (E_MLP, I, H), dtype=jnp.float32) * s_i, 'conv_w': jax.random.normal(ks[5], (KC, 1, H), dtype=jnp.float32) * (1.0 / np.sqrt(KC)), 'conv_b': jnp.zeros((H,), dtype=jnp.float32)}
    _L0_ffn_in = _L0_ffn_setup()
    _d = {'L0_attn_x': _L0_attn_in['x'], 'L0_attn_wq': _L0_attn_in['wq'], 'L0_attn_wk': _L0_attn_in['wk'], 'L0_attn_wv': _L0_attn_in['wv'], 'L0_attn_wo': _L0_attn_in['wo'], 'L0_ffn_Wr': _L0_ffn_in['Wr'], 'L0_ffn_router_bias': _L0_ffn_in['router_bias'], 'L0_ffn_Wg': _L0_ffn_in['Wg'], 'L0_ffn_Wu': _L0_ffn_in['Wu'], 'L0_ffn_Wd': _L0_ffn_in['Wd'], 'L0_ffn_conv_w': _L0_ffn_in['conv_w'], 'L0_ffn_conv_b': _L0_ffn_in['conv_b']}
    _x0 = _d['L0_attn_x']
    _d['L0_attn_x'] = jax.random.normal(jax.random.fold_in(jax.random.key(seed), 1), (8, 2048, 256), dtype=_x0.dtype)
    del _x0
    return _d

def reference(L0_attn_x, L0_attn_wq, L0_attn_wk, L0_attn_wv, L0_attn_wo, L0_ffn_Wr, L0_ffn_router_bias, L0_ffn_Wg, L0_ffn_Wu, L0_ffn_Wd, L0_ffn_conv_w, L0_ffn_conv_b):

    def _L0_attn_ref(x, wq, wk, wv, wo):
        import jax, jax.numpy as jnp
        import numpy as np
        import math
        B, N, E, D = (4, 2048, 256, 64)
        Q = jnp.einsum('bne,de->bnd', x, wq)
        K = jnp.einsum('bne,de->bnd', x, wk)
        V = jnp.einsum('bne,de->bnd', x, wv)
        energy = jnp.einsum('bnd,bne->bde', K, V)
        context = jnp.einsum('bnd,bde->bne', Q, energy)
        context = context * jnp.asarray(math.sqrt(3.0 / D), dtype=context.dtype)
        out = jnp.einsum('bnd,ed->bne', context, wo)
        return out

    def _L0_ffn_ref(hidden_states, Wr, router_bias, Wg, Wu, Wd, conv_w, conv_b):
        import jax, jax.numpy as jnp
        import numpy as np
        from jax import lax
        H = 256
        E = 8
        E_MLP = E - 4
        TOP_K = 2
        I = 128
        KC = 4
        SHARED_SCALE = 1.0
        B, S, Hd = hidden_states.shape
        T = B * S
        x = hidden_states.reshape(T, Hd)
        scores = jax.nn.sigmoid(x @ Wr)
        _, idx = lax.top_k(scores + router_bias, TOP_K)
        w = jnp.take_along_axis(scores, idx, axis=-1)
        w = w / (jnp.sum(w, axis=-1, keepdims=True) + 1e-09)
        cw = jnp.zeros((T, E), dtype=x.dtype).at[jnp.arange(T)[:, None], idx].add(w)
        g = jnp.einsum('th,ehi->tei', x, Wg)
        u = jnp.einsum('th,ehi->tei', x, Wu)
        hid = jax.nn.silu(g) * u
        mlp_out = jnp.einsum('tei,eih->teh', hid, Wd)
        routed = jnp.einsum('te,teh->th', cw[:, :E_MLP], mlp_out)
        routed = routed + cw[:, E_MLP:E_MLP + 1] * x
        routed = routed + cw[:, E_MLP + 2:E_MLP + 3] * x
        routed = routed + cw[:, E_MLP + 3:E_MLP + 4] * jax.nn.relu(x)
        routed = routed.reshape(B, S, Hd)
        shared = lax.conv_general_dilated(hidden_states, conv_w, window_strides=(1,), padding=[(KC - 1, 0)], dimension_numbers=('NHC', 'HIO', 'NHC'), feature_group_count=Hd) + conv_b
        return routed + SHARED_SCALE * shared
    x = L0_attn_x
    x = x + _L0_attn_ref(_layernorm(x, axis=-1), L0_attn_wq, L0_attn_wk, L0_attn_wv, L0_attn_wo)
    x = x + _L0_ffn_ref(_layernorm(x, axis=-1), L0_ffn_Wr, L0_ffn_router_bias, L0_ffn_Wg, L0_ffn_Wu, L0_ffn_Wd, L0_ffn_conv_w, L0_ffn_conv_b)
    return x

_drawn_inputs = setup_inputs


def setup_inputs(seed=0):
    import zlib

    import numpy as np

    out = dict(_drawn_inputs(seed))
    spreads = {'L0_ffn_router_bias': (0.0, 0.8), 'L0_ffn_conv_b': (0.0, 0.8)}
    factors = {'L0_ffn_Wr': 8.0,
     'L0_ffn_Wg': 8.0,
     'L0_ffn_Wu': 8.0,
     'L0_ffn_Wd': 8.0,
     'L0_ffn_conv_w': 8.0}
    for name, (base, spread) in spreads.items():
        noise = np.random.default_rng([zlib.crc32(name.encode()), seed]).standard_normal(out[name].shape)
        drawn = base * np.exp(spread * noise) if base else spread * noise
        out[name] = jnp.asarray(drawn.astype(out[name].dtype))
    for name, factor in factors.items():
        out[name] = (out[name] * factor).astype(out[name].dtype)
    return out
```

```python
import math
from contextlib import ExitStack

import concourse.bass as bass
from concourse import mybir

F32 = mybir.dt.float32
F32R = mybir.dt.float32r
U32 = mybir.dt.uint32
ALU = mybir.AluOpType
ACT = mybir.ActivationFunctionType
AXX = mybir.AxisListType.X

P = 128
LAG = {"L": 0, "A": 1, "X": 4, "B": 5, "R": 6, "C": 7, "Y": 8}
UNROLL = 4
EPS_LN = 1e-5
EPS_W = 1e-9


class Step:

    def __init__(self, r, s, groups):
        self.r, self.s, self.groups = r, s, groups
        self.peeled = isinstance(r, int)

    def on(self, stage):
        return not self.peeled or 0 <= UNROLL * self.r + self.s - LAG[stage] < self.groups

    def was_on(self, stage):
        return not self.peeled or 0 <= UNROLL * self.r + self.s - 1 - LAG[stage] < self.groups

    def later(self, stage, n):
        return not self.peeled or UNROLL * self.r + self.s - LAG[stage] >= n

    def first(self, stage):
        return (self.s - LAG[stage]) % UNROLL == 0

    def last(self, stage):
        return (self.s - LAG[stage]) % UNROLL == UNROLL - 1

    def group(self, stage):
        return UNROLL * self.r + (self.s - LAG[stage])

    def slot(self, stage, n):
        return (self.s - LAG[stage]) % n

    def before(self, stage, per=1, extra=0):
        n = self.s - LAG[stage]
        if self.peeled:
            return per * min(max(UNROLL * self.r + n, 0), self.groups) + extra
        return self.r * (UNROLL * per) + (n * per + extra)

    def uses(self, stage, n, per=1, extra=0):
        k = (self.s - LAG[stage]) // n
        return self.r * (UNROLL // n * per) + (k * per + extra)

    def chains(self, per=1, extra=0):
        k = (self.s - LAG["B"] - 1) // UNROLL + 1
        if self.peeled:
            return per * min(max(self.r + k, 0), self.groups // UNROLL) + extra
        return self.r * per + (k * per + extra)

    def chain(self):
        return self.first("B") and self.on("B")


GU_BANK = [k % 3 for k in range(8)]


def program(nc, x, wq, wkT, wvT, woT, wr, rbias, wg, wu, wd, convwb, cw_rows, out):
    T, H = x.shape
    D = wq.shape[0]
    NE = wr.shape[1]
    EM, _, I = wg.shape
    KC = convwb.shape[1] - 1
    HC = H // P
    TG = 4
    GT = TG * P
    NG = T // GT
    SCALE = math.sqrt(3.0 / D)
    assert D == 64 and I == P and HC == 2 and NG % UNROLL == 0
    ROUNDS = (NG + max(LAG.values())) // UNROLL
    LOOP = (LAG["Y"] // UNROLL, NG // UNROLL)

    x_rows = x.rearrange("(n p) f -> p n f", p=P)
    out_rows = out.rearrange("(n p) f -> p n f", p=P)

    ctx = ExitStack()
    with ctx:
        def sb(name, shape, dt=F32):
            return ctx.enter_context(nc.sbuf_tensor(name, shape, dt))

        def bank(name):
            return ctx.enter_context(nc.psum_tensor(name, [P, 512], F32))

        def sem(name):
            return ctx.enter_context(nc.semaphore(name))

        wq_sb = sb("wq_sb", [D, H])
        wkT_sb = sb("wkT_sb", [P, HC, D])
        wvT_sb = sb("wvT_sb", [P, HC, D])
        woT_sb = sb("woT_sb", [D, H])
        wr_sb = sb("wr_sb", [P, HC, NE])
        wr_hi = sb("wr_hi", [P, HC, NE], F32R)
        wr_lo = sb("wr_lo", [P, HC, NE], F32R)
        wgu_hi = sb("wgu_hi", [P, 2, EM, HC, I], F32R)
        wgu_lo = sb("wgu_lo", [P, 2, EM, HC, I], F32R)
        wd_hi = sb("wd_hi", [P, EM, H], F32R)
        wd_lo = sb("wd_lo", [P, EM, H], F32R)
        conv_w = sb("conv_w", [P, HC, KC + 1])
        bias8 = sb("bias8", [P, TG, NE])
        ident = sb("ident", [P, P])
        iota_u = sb("iota_u", [P, NE], U32)
        iota_f = sb("iota_f", [P, NE])
        tick = sb("tick", [1, 1])
        eps_ln = sb("eps_ln", [P, TG])
        half_neg = sb("half_neg", [P, TG])
        inv_e = sb("inv_e", [P, TG * NE])

        xa = sb("xa", [P, 2, TG, H])
        stats1 = sb("stats1", [P, TG, 6])
        mv1 = sb("mv1", [P, TG, 2])
        rstd1 = sb("rstd1", [P, TG])
        xn = sb("xn", [P, 2, TG, H])
        xn_hi = sb("xn_hi", [P, TG, H], F32R)
        xn_lo = sb("xn_lo", [P, TG, H], F32R)
        xnT_hi = sb("xnT_hi", [P, 4, HC, GT], F32R)
        xnT_lo = sb("xnT_lo", [P, 4, HC, GT], F32R)
        gram = sb("gram", [P, HC, H])
        p1 = sb("p1", [P, HC, D])
        et = sb("et", [D, D])
        ff = sb("ff", [D, H])
        m_hi = sb("m_hi", [P, HC, H], F32R)
        m_lo = sb("m_lo", [P, HC, H], F32R)
        acc = sb("acc", [P, 4, TG, H])
        stats2 = sb("stats2", [P, TG, 6])
        mv2 = sb("mv2", [P, TG, 2])
        rstd2 = sb("rstd2", [P, TG])
        x2 = sb("x2", [P, 2, TG, H])
        PAD = KC - 1
        x2T = sb("x2T", [P, 2, HC, PAD + GT])
        x2T_hi = sb("x2T_hi", [P, 2, HC, GT], F32R)
        x2T_lo = sb("x2T_lo", [P, 2, HC, GT], F32R)
        logits = sb("logits", [P, TG * NE])
        enx = sb("enx", [P, TG * NE])
        den = sb("den", [P, TG * NE])
        score = sb("score", [P, TG, NE])
        biased = sb("biased", [P, TG, NE])
        top8 = sb("top8", [P, TG, 8])
        idx8 = sb("idx8", [P, TG, 8], U32)
        idxf = sb("idxf", [P, TG, 2])
        hot = sb("hot", [P, 2, TG, NE])
        chosen = sb("chosen", [P, TG, NE])
        raw = sb("raw", [P, TG, NE])
        wsum = sb("wsum", [P, TG])
        wsum_eps = sb("wsum_eps", [P, TG])
        winv = sb("winv", [P, TG])
        cw = sb("cw", [P, 2, TG, NE])
        coef = sb("coef", [P, 2, TG])
        cwT = sb("cwT", [EM, GT])
        cwb = sb("cwb", [P, 2, EM, GT])
        gate = sb("gate", [P, 2, GT])
        hid = sb("hid", [P, 2, GT])
        hid_hi = sb("hid_hi", [P, 2, GT], F32R)
        hid_lo = sb("hid_lo", [P, 2, GT], F32R)
        conv = sb("conv", [P, 2, HC, GT])
        w_stage = cwb[:, :, :, :].rearrange("p a e n -> p (a e n)")
        wg_st = w_stage[:, 0:EM * HC * I].rearrange("p (e c i) -> p e c i", e=EM, c=HC)
        wu_st = w_stage[:, EM * HC * I:2 * EM * HC * I].rearrange("p (e c i) -> p e c i", e=EM, c=HC)
        wd_st = w_stage[:, 2 * EM * HC * I:2 * EM * HC * I + EM * H].rearrange("p (e n) -> p e n", e=EM)

        ps_gram = bank("ps_gram")
        ps_gu = [bank(f"ps_gu{k}") for k in range(3)]
        ps_y = [bank(f"ps_y{c}") for c in range(HC)]
        ps_sh = [bank(f"ps_sh{k}") for k in range(2)]

        w_loaded = sem("w_loaded")
        xa_loaded = [sem(f"xa_loaded{k}") for k in range(2)]
        acc_loaded = [sem(f"acc_loaded{k}") for k in range(4)]
        out_stored = [sem(f"out_stored{k}") for k in range(4)]
        cw_stored = sem("cw_stored")
        cwb_loaded = [sem(f"cwb_loaded{k}") for k in range(2)]
        zeroed = sem("zeroed")
        ident_ready = sem("ident_ready")
        const_ready = sem("const_ready")
        iota_ready = sem("iota_ready")
        iotaf_ready = sem("iotaf_ready")
        whi_ready = sem("whi_ready")
        wlo_ready = sem("wlo_ready")
        stat1 = sem("stat1")
        aggr1 = sem("aggr1")
        veps1 = sem("veps1")
        rstd1_ready = sem("rstd1_ready")
        xn_ready = sem("xn_ready")
        xnhi_ready = sem("xnhi_ready")
        xnlo_ready = sem("xnlo_ready")
        gram_done = sem("gram_done")
        gram_out = sem("gram_out")
        gramT_done, gramT_out = sem("gramT_done"), sem("gramT_out")
        p1_done, p1_out = sem("p1_done"), sem("p1_out")
        et_done, et_out = sem("et_done"), sem("et_out")
        f_done, f_out = sem("f_done"), sem("f_out")
        m_done, mhi_out, mlo_out = sem("m_done"), sem("mhi_out"), sem("mlo_out")
        xnT_done = sem("xnT_done")
        xnThi_ready = sem("xnThi_ready")
        xnTlo_ready = sem("xnTlo_ready")
        attn_done = sem("attn_done")
        x1_ready = sem("x1_ready")
        stat2 = sem("stat2")
        aggr2 = sem("aggr2")
        veps2 = sem("veps2")
        rstd2_ready = sem("rstd2_ready")
        x2_ready = sem("x2_ready")
        x2T_done = sem("x2T_done")
        x2T_ready = sem("x2T_ready")
        x2Thi_ready = sem("x2Thi_ready")
        x2Tlo_ready = sem("x2Tlo_ready")
        halo_ready = sem("halo_ready")
        router_done = sem("router_done")
        logits_ready = sem("logits_ready")
        enx_ready = sem("enx_ready")
        rt = sem("rt")
        cw_ready = sem("cw_ready")
        cwT_done = sem("cwT_done")
        cwT_ready = sem("cwT_ready")
        gu_done = sem("gu_done")
        gate_ready = sem("gate_ready")
        gatew_ready = sem("gatew_ready")
        hid_ready = sem("hid_ready")
        hidhi_ready = sem("hidhi_ready")
        hidlo_ready = sem("hidlo_ready")
        down_done = sem("down_done")
        tap_ready = sem("tap_ready")
        conv_ready = sem("conv_ready")
        ident_added = sem("ident_added")
        relu_ready = sem("relu_ready")
        relu_added = sem("relu_added")
        ysum_ready = sem("ysum_ready")
        y_done = sem("y_done")
        out_ready = sem("out_ready")

        CT = HC * PAD
        N_LOADS = 6 + TG + 2 * EM + 1
        NSPLIT = 4

        def steps(eng, body):
            for r in range(LOOP[0]):
                for s in range(UNROLL):
                    body(Step(r, s, NG))
            with eng.Fori(LOOP[0], LOOP[1], 1) as r:
                for s in range(UNROLL):
                    body(Step(r, s, NG))
            for r in range(LOOP[1], ROUNDS):
                for s in range(UNROLL):
                    body(Step(r, s, NG))

        block = ctx.enter_context(nc.Block())

        @block.sync
        def _(sp):
            def load_x(st):
                if st.later("L", 2):
                    sp.wait_ge(xn_ready, st.before("L", TG, -TG))
                sp.dma_start(xa[:, st.slot("L", 2)], x_rows[:, bass.ds(st.group("L") * TG, TG), :])\
                    .then_inc(xa_loaded[st.slot("L", 2)], 16)

            load_x(Step(0, 0, NG))
            sp.dma_start(wq_sb[:, :], wq).then_inc(w_loaded, 16)
            sp.dma_start(wkT_sb[:, :, :], wkT.rearrange("(c p) d -> p c d", p=P)).then_inc(w_loaded, 16)
            sp.dma_start(wvT_sb[:, :, :], wvT.rearrange("(c p) d -> p c d", p=P)).then_inc(w_loaded, 16)
            sp.dma_start(woT_sb[:, :], woT).then_inc(w_loaded, 16)
            sp.dma_start(wr_sb[:, :, :], wr.rearrange("(c p) e -> p c e", p=P)).then_inc(w_loaded, 16)
            sp.dma_start(conv_w[:, :, :], convwb.rearrange("(c p) k -> p c k", p=P)).then_inc(w_loaded, 16)
            for t in range(TG):
                sp.dma_start(bias8[:, t, :], rbias.partition_broadcast(P)).then_inc(w_loaded, 16)
            for e in range(EM):
                sp.dma_start(wg_st[:, e], wg[e].rearrange("(c p) i -> p c i", p=P)).then_inc(w_loaded, 16)
                sp.dma_start(wu_st[:, e], wu[e].rearrange("(c p) i -> p c i", p=P)).then_inc(w_loaded, 16)
            sp.dma_start(wd_st, wd.rearrange("e i n -> i e n")).then_inc(w_loaded, 16)

            def body(st):
                if st.on("L") and not (st.peeled and st.r == 0 and st.s == 0):
                    load_x(st)
                if st.on("Y"):
                    k = st.slot("Y", 4)
                    for h in range(2):
                        sp.wait_ge(out_ready, st.before("Y", 2, h + 1))
                        sp.dma_start(out_rows[:, bass.ds(st.group("Y") * TG + 2 * h, 2), :],
                                     acc[:, k, 2 * h:2 * h + 2]).then_inc(out_stored[k], 16)
                if st.on("R"):
                    k = st.slot("R", 2)
                    rows = cw_rows[bass.ds(st.group("R"), 1)]
                    sp.wait_ge(cwT_ready, st.before("R", 1, 1))
                    sp.dma_start(rows.rearrange("a e n -> (a e) n"), cwT[:, :]).then_inc(cw_stored, 16)
                    sp.wait_ge(cw_stored, st.before("R", 16, 16))
                    if st.peeled and st.before("R") < 2:
                        sp.wait_ge(whi_ready, NSPLIT)
                        sp.wait_ge(wlo_ready, NSPLIT)
                    sp.dma_start(cwb[:, k].rearrange("p e n -> p (e n)"),
                                 rows.rearrange("a e n -> (a e n)").partition_broadcast(P))\
                        .then_inc(cwb_loaded[k], 16)
                if st.on("X"):
                    k = st.slot("X", 4)
                    if st.later("X", 4):
                        sp.wait_ge(out_stored[k], st.uses("X", 4, 32))
                    sp.dma_start(acc[:, k], x_rows[:, bass.ds(st.group("X") * TG, TG), :])\
                        .then_inc(acc_loaded[k], 16)

            steps(sp, body)
            for k in range(4):
                sp.wait_ge(out_stored[k], 32 * (NG // 4))
            sp.wait_ge(cw_stored, 16 * NG)

        @block.tensor
        def _(pe):
            def three(dst, a_hi, a_lo, b_hi, b_lo, start, stop):
                nc.tensor.matmul(dst, a_hi, b_hi, start=start, stop=False, skip_group_check=True)
                nc.tensor.matmul(dst, a_hi, b_lo, start=False, stop=False, skip_group_check=True)
                return nc.tensor.matmul(dst, a_lo, b_hi, start=False, stop=stop, skip_group_check=True)

            def gate_up(st, k):
                e, w = divmod(k, 2)
                q = st.slot("C", 2)
                if k == 0:
                    pe.wait_ge(x2Tlo_ready, st.before("C", HC, HC))
                if k >= 3:
                    ke, kw = divmod(k - 3, 2)
                    pe.wait_ge((gate_ready, hid_ready)[kw], st.before("C", EM, ke + 1))
                else:
                    ke, kw = divmod((6, 7, 5)[k], 2)
                    if st.later("C", 1):
                        pe.wait_ge((gate_ready, hid_ready)[kw], st.before("C", EM, ke + 1 - EM))
                for c in range(HC):
                    last = three(ps_gu[GU_BANK[k]][:, :], wgu_hi[:, w, e, c], wgu_lo[:, w, e, c],
                                 x2T_hi[:, q, c], x2T_lo[:, q, c], c == 0, c == HC - 1)
                last.then_inc(gu_done, 1)

            def down(st, stage, e):
                pe.wait_ge(hidlo_ready, st.before(stage, EM, e + 1))
                if e == 0:
                    if st.later(stage, 1):
                        pe.wait_ge(ysum_ready, st.before(stage, HC))
                h = e % 2
                for c in range(HC):
                    last = three(ps_y[c][:, :], wd_hi[:, e, c * P:(c + 1) * P], wd_lo[:, e, c * P:(c + 1) * P],
                                 hid_hi[:, h], hid_lo[:, h], e == 0, e == EM - 1)
                last.then_inc(down_done, 1)

            def gram_matrix(st):
                pe.wait_ge(xnlo_ready, st.before("A", 1, 1))
                if st.first("A") and st.chain():
                    pe.wait_ge(gram_out, st.chains(2, 2))
                for t in range(TG):
                    start = st.first("A") and t == 0
                    stop = st.last("A") and t == TG - 1
                    three(ps_gram[:, 0:H], xn_hi[:, t, 0:P], xn_lo[:, t, 0:P],
                          xn_hi[:, t, :], xn_lo[:, t, :], start, stop)
                    last = three(ps_gram[:, H:H + P], xn_hi[:, t, P:H], xn_lo[:, t, P:H],
                                 xn_hi[:, t, P:H], xn_lo[:, t, P:H], False, stop)
                last.then_inc(gram_done, 1)

            def xn_transpose(st, c):
                if c == 0 and st.on("B"):
                    pe.wait_ge(x1_ready, st.before("B", 2, 2))
                elif c == 1 and st.on("R"):
                    pe.wait_ge(cwT_ready, st.before("R", 1, 1))
                elif c == 1 and st.on("B"):
                    pe.wait_ge(x1_ready, st.before("B", 2, 1))
                elif st.later("A", 1):
                    pe.wait_ge(xnTlo_ready, st.before("A", HC))
                b = ps_sh[c]
                for t in range(TG):
                    last = nc.tensor.transpose(b[:, t * P:(t + 1) * P],
                                               xn[:, st.slot("A", 2), t, c * P:(c + 1) * P], ident[:, :])
                last.then_inc(xnT_done, 1)

            def x2_transpose(st, c):
                if c == 0:
                    pe.wait_ge(x2_ready, st.before("R", TG, TG))
                if c == 1:
                    pe.wait_ge(x2Thi_ready, st.before("R", HC, 1))
                elif st.was_on("A"):
                    pe.wait_ge(xnTlo_ready, st.before("A", HC, -1))
                else:
                    pe.wait_ge(x1_ready, st.before("B", 2))
                b = ps_sh[0]
                for t in range(TG):
                    last = nc.tensor.transpose(b[:, t * P:(t + 1) * P],
                                               x2[:, st.slot("R", 2), t, c * P:(c + 1) * P], ident[:, :])
                last.then_inc(x2T_done, 1)

            def router(st):
                pe.wait_ge(x2Tlo_ready, st.before("R", HC, HC))
                if st.on("Y"):
                    pe.wait_ge(out_ready, st.before("Y", 2, 1))
                b, q = ps_sh[0], st.slot("R", 2)
                for t in range(TG):
                    tok = slice(t * P, (t + 1) * P)
                    for c in range(HC):
                        last = three(b[:, t * NE:(t + 1) * NE], x2T_hi[:, q, c, tok], x2T_lo[:, q, c, tok],
                                     wr_hi[:, c], wr_lo[:, c], c == 0, c == HC - 1)
                last.then_inc(router_done, 1)

            def attention(st, h):
                if h == 0 and st.chain():
                    pe.wait_ge(mlo_out, st.chains(1, 1))
                if h == 0:
                    pe.wait_ge(xnTlo_ready, st.before("B", HC, HC))
                if h == 1 and st.on("Y"):
                    pe.wait_ge(out_ready, st.before("Y", 2, 2))
                elif h == 1 and st.on("R"):
                    pe.wait_ge(logits_ready, st.before("R", 1, 1))
                elif h == 1:
                    pe.wait_ge(xnTlo_ready, st.before("A", HC, -1))
                elif not st.chain() and st.was_on("A"):
                    pe.wait_ge(xnTlo_ready, st.before("A", HC))
                elif not st.chain():
                    pe.wait_ge(cwT_ready, st.before("R"))
                b, q = ps_sh[1 - h], st.slot("B", 4)
                for k in range(2):
                    tok = slice((2 * h + k) * P, (2 * h + k + 1) * P)
                    for c in range(HC):
                        last = three(b[:, k * H:(k + 1) * H], xnT_hi[:, q, c, tok], xnT_lo[:, q, c, tok],
                                     m_hi[:, c], m_lo[:, c], c == 0, c == HC - 1)
                last.then_inc(attn_done, 1)

            def weights_transpose(st):
                pe.wait_ge(cw_ready, st.before("R", 1, 1))
                if st.on("B"):
                    pe.wait_ge(x1_ready, st.before("B", 2, 1))
                else:
                    pe.wait_ge(cwT_ready, st.before("R"))
                b = ps_sh[1]
                for t in range(TG):
                    last = nc.tensor.transpose(b[0:EM, t * P:(t + 1) * P], cw[:, st.slot("R", 2), t, 0:EM],
                                               ident[:, :])
                last.then_inc(cwT_done, 1)

            def y_transpose(st, h):
                if h == 0:
                    pe.wait_ge(ysum_ready, st.before("Y", HC, HC))
                if h == 0 and st.on("R"):
                    pe.wait_ge(x2Thi_ready, st.before("R", HC, HC))
                elif h == 0:
                    pe.wait_ge(out_ready, st.before("Y", 2))
                elif st.on("R"):
                    pe.wait_ge(logits_ready, st.before("R", 1, 1))
                else:
                    pe.wait_ge(out_ready, st.before("Y", 2, 1))
                b, q = ps_sh[0], st.slot("Y", 2)
                for k in range(2):
                    t = 2 * h + k
                    for c in range(HC):
                        last = nc.tensor.transpose(b[:, (k * HC + c) * P:(k * HC + c + 1) * P],
                                                   conv[:, q, c, t * P:(t + 1) * P], ident[:, :])
                last.then_inc(y_done, 1)

            def chain_gramT(st):
                pe.wait_ge(gram_out, st.chains(2, 2))
                pe.wait_ge(xnTlo_ready, st.before("A", HC))
                b = ps_sh[1]
                nc.tensor.transpose(b[:, 0:P], gram[:, 0, P:H], ident[:, :]).then_inc(gramT_done, 1)

            def chain_p1(st):
                pe.wait_ge(gramT_out, st.chains(1, 1))
                b = ps_sh[1]
                for m in range(HC):
                    for c in range(HC):
                        last = nc.tensor.matmul(b[:, m * D:(m + 1) * D], gram[:, c, m * P:(m + 1) * P], wvT_sb[:, c],
                                                start=(c == 0), stop=(c == HC - 1))
                last.then_inc(p1_done, 1)

            def chain_et(st):
                pe.wait_ge(p1_out, st.chains(1, 1))
                b = ps_sh[1]
                for c in range(HC):
                    last = nc.tensor.matmul(b[0:D, 0:D], p1[:, c], wkT_sb[:, c], start=(c == 0), stop=(c == HC - 1))
                last.then_inc(et_done, 1)

            def chain_f(st):
                b = ps_sh[1]
                nc.tensor.matmul(b[0:D, 0:H], et[:, :], woT_sb[:, :], start=True, stop=True).then_inc(f_done, 1)

            def chain_m(st):
                pe.wait_ge(f_out, st.chains(1, 1))
                b = ps_sh[1]
                for c in range(HC):
                    last = nc.tensor.matmul(b[:, c * H:(c + 1) * H], wq_sb[:, c * P:(c + 1) * P], ff[:, :],
                                            start=True, stop=True)
                last.then_inc(m_done, 1)

            pe.wait_ge(ident_ready, 1)
            pe.wait_ge(w_loaded, 16 * N_LOADS)
            pe.wait_ge(whi_ready, NSPLIT)
            pe.wait_ge(wlo_ready, NSPLIT)

            def body(st):
                c_on, y_on, r_on, m_on = st.on("C"), st.on("Y"), st.on("R"), st.chain()
                if c_on:
                    gate_up(st, 0)
                if r_on:
                    x2_transpose(st, 0)
                if m_on:
                    chain_gramT(st)
                if y_on:
                    down(st, "Y", EM - 1)
                if c_on:
                    gate_up(st, 1)
                if r_on:
                    x2_transpose(st, 1)
                if m_on:
                    chain_p1(st)
                if c_on:
                    gate_up(st, 2)
                if m_on:
                    chain_et(st)
                if c_on:
                    gate_up(st, 3)
                if m_on:
                    pe.wait_ge(et_out, st.chains(1, 1))
                if y_on:
                    y_transpose(st, 0)
                if m_on:
                    chain_f(st)
                if c_on:
                    down(st, "C", 0)
                if r_on:
                    router(st)
                if m_on:
                    chain_m(st)
                if y_on:
                    y_transpose(st, 1)
                if c_on:
                    gate_up(st, 4)
                if st.on("A"):
                    gram_matrix(st)
                if c_on:
                    gate_up(st, 5)
                    down(st, "C", 1)
                if st.on("B"):
                    attention(st, 0)
                if r_on:
                    weights_transpose(st)
                if c_on:
                    gate_up(st, 6)
                if st.on("B"):
                    attention(st, 1)
                if c_on:
                    gate_up(st, 7)
                    down(st, "C", 2)
                if st.on("A"):
                    xn_transpose(st, 0)
                    xn_transpose(st, 1)

            steps(pe, body)

        @block.scalar
        def _(act):
            def copy(dst, src, scale=1.0):
                return nc.scalar.activation(dst, src, ACT.Copy, scale=scale)

            def silu(st, e):
                act.wait_ge(gu_done, st.before("C", 2 * EM, 2 * e + 1))
                if st.later("C", 1) or e > 1:
                    act.wait_ge(hid_ready, st.before("C", EM, e - 1))
                nc.scalar.activation(gate[:, e % 2], ps_gu[GU_BANK[2 * e]][:, :], ACT.Silu)\
                    .then_inc(gate_ready, 1)

            def hid_high(st, e):
                act.wait_ge(hid_ready, st.before("C", EM, e + 1))
                if st.later("C", 1) or e > 1:
                    act.wait_ge(down_done, st.before("C", EM, e - 1))
                copy(hid_hi[:, e % 2], hid[:, e % 2]).then_inc(hidhi_ready, 1)

            def x2T_out(st, c):
                act.wait_ge(x2T_done, st.before("R", HC, c + 1))
                q = st.slot("R", 2)
                if c == 0:
                    if st.later("R", 2):
                        act.wait_ge(conv_ready, st.before("R", CT, -CT))
                    if st.later("R", 1):
                        act.wait_ge(halo_ready, st.before("R"))
                    if st.later("R", 2):
                        act.wait_ge(gu_done, st.before("R", 2 * EM, -2 * EM))
                    if st.later("R", 2):
                        act.wait_ge(x2Tlo_ready, st.before("R", HC, -HC))
                copy(x2T[:, q, c, PAD:PAD + GT], ps_sh[0][:, :]).then_inc(x2T_ready, 1)
                copy(x2T_hi[:, q, c], ps_sh[0][:, :]).then_inc(x2Thi_ready, 1)

            def chain_copy(st, done, count, pairs, out_sem, scale=1.0):
                act.wait_ge(done, count)
                for dst, src in pairs:
                    copy(dst, src, scale).then_inc(out_sem, 1)

            act.wait_ge(w_loaded, 16 * N_LOADS)
            copy(wgu_hi[:, 0].rearrange("p e c i -> p (e c i)"), wg_st.rearrange("p e c i -> p (e c i)"))\
                .then_inc(whi_ready, 1)
            copy(wgu_hi[:, 1].rearrange("p e c i -> p (e c i)"), wu_st.rearrange("p e c i -> p (e c i)"))\
                .then_inc(whi_ready, 1)
            copy(wd_hi[:, :, :], wd_st).then_inc(whi_ready, 1)
            copy(wr_hi[:, :, :], wr_sb[:, :, :]).then_inc(whi_ready, 1)

            def body(st):
                c_on, r_on, m_on = st.on("C"), st.on("R"), st.chain()
                if m_on:
                    chain_copy(st, gram_done, st.before("A"),
                               [(gram[:, 0, :], ps_gram[:, 0:H]), (gram[:, 1, P:H], ps_gram[:, H:H + P])], gram_out)
                if c_on:
                    silu(st, 0)
                    q = st.slot("C", 2)
                    act.wait_ge(x2T_ready, st.before("C", HC, HC))
                    if st.later("C", 2):
                        act.wait_ge(y_done, st.before("C", 2, -2))
                    for c in range(HC):
                        nc.scalar.activation(conv[:, q, c], x2T[:, q, c, PAD:PAD + GT], ACT.Identity,
                                             bias=conv_w[:, c, KC:KC + 1], scale=conv_w[:, c, PAD:PAD + 1])\
                            .then_inc(tap_ready, 1)
                if r_on:
                    x2T_out(st, 0)
                if m_on:
                    chain_copy(st, gramT_done, st.chains(1, 1), [(gram[:, 1, 0:P], ps_sh[1][:, 0:P])], gramT_out)
                if c_on:
                    hid_high(st, 0)
                if r_on:
                    x2T_out(st, 1)
                if m_on:
                    chain_copy(st, p1_done, st.chains(1, 1),
                               [(p1[:, :, :], ps_sh[1][:, 0:HC * D].rearrange("p (c d) -> p c d", c=HC))], p1_out)
                if c_on:
                    silu(st, 1)
                if m_on:
                    chain_copy(st, et_done, st.chains(1, 1), [(et[:, :], ps_sh[1][0:D, 0:D])], et_out)
                if c_on:
                    hid_high(st, 1)
                if m_on:
                    chain_copy(st, f_done, st.chains(1, 1), [(ff[:, :], ps_sh[1][0:D, 0:H])], f_out, SCALE)
                if c_on:
                    q = st.slot("C", 2)
                    for t in range(TG):
                        act.wait_ge(ident_added, st.before("C", TG, t + 1))
                        nc.scalar.activation(x2[:, q, t], x2[:, q, t], ACT.Relu, scale=cw[:, q, t, EM + 3:EM + 4])\
                            .then_inc(relu_ready, 1)
                if m_on:
                    chain_copy(st, m_done, st.chains(1, 1),
                               [(m_hi[:, :, :], ps_sh[1][:, :].rearrange("p (c n) -> p c n", c=HC))], mhi_out)
                if c_on:
                    silu(st, 2)
                if st.on("L"):
                    act.wait_ge(xn_ready, st.before("L", TG, TG))
                    if st.later("L", 1):
                        act.wait_ge(gram_done, st.before("L"))
                    copy(xn_hi[:, :, :], xn[:, st.slot("L", 2)]).then_inc(xnhi_ready, 1)
                if c_on:
                    hid_high(st, 2)
                if r_on:
                    act.wait_ge(cwT_done, st.before("R", 1, 1))
                    if st.later("R", 1):
                        act.wait_ge(cw_stored, st.before("R", 16))
                    copy(cwT[:, :], ps_sh[1][0:EM, :]).then_inc(cwT_ready, 1)
                if c_on:
                    silu(st, 3)
                    hid_high(st, 3)
                if st.on("A"):
                    for c in range(HC):
                        act.wait_ge(xnT_done, st.before("A", HC, c + 1))
                        copy(xnT_hi[:, st.slot("A", 4), c], ps_sh[c][:, :]).then_inc(xnThi_ready, 1)

            steps(act, body)

        @block.vector
        def _(dve):
            v = nc.vector

            def turn(sem, count):
                dve.wait_ge(sem, count)
                v.tensor_copy(tick[:, :], iota_f[0:1, 0:1])

            def hidden(st, e):
                dve.wait_ge(gatew_ready, st.before("C", EM, e + 1))
                dve.wait_ge(gu_done, st.before("C", 2 * EM, 2 * e + 2))
                if st.later("C", 1) or e > 1:
                    dve.wait_ge(hidlo_ready, st.before("C", EM, e - 1))
                v.tensor_tensor(hid[:, e % 2], ps_gu[GU_BANK[2 * e + 1]][:, :], gate[:, e % 2], ALU.mult)\
                    .then_inc(hid_ready, 1)

            def conv_tap(st, n):
                q, k = st.slot("C", 2), PAD - 1 - n
                for c in range(HC):
                    if n == 0:
                        dve.wait_ge(tap_ready, st.before("C", HC, c + 1))
                    else:
                        dve.wait_ge(conv_ready, st.before("C", CT, HC * (n - 1) + c + 1))
                    v.scalar_tensor_tensor(conv[:, q, c], x2T[:, q, c, k:k + GT], conv_w[:, c, k:k + 1],
                                           conv[:, q, c], ALU.mult, ALU.add).then_inc(conv_ready, 1)

            def norm1_stats(st):
                q = st.slot("L", 2)
                dve.wait_ge(xa_loaded[q], st.uses("L", 2, 16, 16))
                for t in range(TG):
                    v.bn_stats(stats1[:, t], xa[:, q, t]).then_inc(stat1, 1)
                turn(stat1, st.before("L", TG, TG))
                for t in range(TG):
                    v.bn_aggr(mv1[:, t], stats1[:, t]).then_inc(aggr1, 1)

            def norm1(st):
                q = st.slot("L", 2)
                dve.wait_ge(rstd1_ready, st.before("L", 1, 1))
                if st.later("L", 2):
                    dve.wait_ge(xnT_done, st.before("L", HC, -HC))
                if st.later("L", 2):
                    dve.wait_ge(xnlo_ready, st.before("L", 1, -1))
                for t in range(TG):
                    v.tensor_scalar(xn[:, q, t], xa[:, q, t], mv1[:, t, 0:1], rstd1[:, t:t + 1],
                                    ALU.subtract, ALU.mult).then_inc(xn_ready, 1)

            def residual(st, h):
                q = st.slot("B", 4)
                dve.wait_ge(attn_done, st.before("B", 2, h + 1))
                if h == 0:
                    dve.wait_ge(acc_loaded[q], st.uses("B", 4, 16, 16))
                two = acc[:, q, 2 * h:2 * h + 2].rearrange("p t n -> p (t n)")
                v.tensor_tensor(two, ps_sh[1 - h][:, :], two, ALU.add).then_inc(x1_ready, 1)

            def norm2_stats(st, h):
                q = st.slot("B", 4)
                dve.wait_ge(x1_ready, st.before("B", 2, h + 1))
                for t in (2 * h, 2 * h + 1):
                    v.bn_stats(stats2[:, t], acc[:, q, t]).then_inc(stat2, 1)
                turn(stat2, st.before("B", TG, 2 * h + 2))
                for t in (2 * h, 2 * h + 1):
                    v.bn_aggr(mv2[:, t], stats2[:, t]).then_inc(aggr2, 1)

            def norm2(st):
                q = st.slot("B", 2)
                dve.wait_ge(rstd2_ready, st.before("B", 1, 1))
                if st.later("B", 2):
                    dve.wait_ge(relu_added, st.before("B", 1, -1))
                if st.later("B", 2):
                    dve.wait_ge(x2T_done, st.before("B", HC, -HC))
                for t in range(TG):
                    v.tensor_scalar(x2[:, q, t], acc[:, st.slot("B", 4), t], mv2[:, t, 0:1], rstd2[:, t:t + 1],
                                    ALU.subtract, ALU.mult).then_inc(x2_ready, 1)

            RT = 12 + 2 * TG

            def flat(t):
                return t.rearrange("p t e -> p (t e)")

            def route(st):
                q = st.slot("R", 2)
                issued = [0]

                def after():
                    dve.wait_ge(rt, st.before("R", RT, issued[0]))

                def done(ins):
                    issued[0] += 1
                    ins.then_inc(rt, 1)

                dve.wait_ge(enx_ready, st.before("R", 1, 1))
                done(v.tensor_scalar(den[:, :], enx[:, :], 1.0, None, ALU.add))
                after()
                done(v.reciprocal(flat(score[:, :, :]), den[:, :]))
                after()
                done(v.tensor_tensor(biased[:, :, :], score[:, :, :], bias8[:, :, :], ALU.add))
                turn(rt, st.before("R", RT, issued[0]))
                for t in range(TG):
                    done(v.max(top8[:, t], biased[:, t]))
                turn(rt, st.before("R", RT, issued[0]))
                for t in range(TG):
                    done(v.max_index(idx8[:, t], top8[:, t], biased[:, t]))
                after()
                done(v.tensor_copy(idxf[:, :, :], idx8[:, :, 0:2]))
                after()
                for n in range(2):
                    done(v.tensor_tensor(hot[:, n], iota_f[:, :].unsqueeze(1).broadcast_to([P, TG, NE]),
                                         idxf[:, :, n:n + 1].broadcast_to([P, TG, NE]), ALU.is_equal))
                after()
                done(v.tensor_tensor(chosen[:, :, :], hot[:, 0], hot[:, 1], ALU.add))
                after()
                done(v.tensor_tensor(raw[:, :, :], chosen[:, :, :], score[:, :, :], ALU.mult))
                after()
                done(v.tensor_reduce(wsum[:, :], raw[:, :, :], AXX, ALU.add))
                after()
                done(v.tensor_scalar(wsum_eps[:, :], wsum[:, :], EPS_W, None, ALU.add))
                after()
                done(v.reciprocal(winv[:, :], wsum_eps[:, :]))
                after()
                if st.later("R", 2):
                    dve.wait_ge(relu_ready, st.before("R", TG, -TG))
                if st.later("R", 2):
                    dve.wait_ge(cwT_done, st.before("R", 1, -1))
                v.tensor_tensor(cw[:, q], raw[:, :, :], winv[:, :].unsqueeze(2).broadcast_to([P, TG, NE]),
                                ALU.mult).then_inc(cw_ready, 1)
                dve.wait_ge(cw_ready, st.before("R", 1, 1))
                done(v.tensor_tensor(coef[:, q], cw[:, q, :, EM], cw[:, q, :, EM + 2], ALU.add))
                assert issued[0] == RT

            dve.wait_ge(w_loaded, 16 * N_LOADS)
            dve.wait_ge(whi_ready, NSPLIT)
            for hi, lo, full in ((wgu_hi[:, 0].rearrange("p e c i -> p (e c i)"),
                                  wgu_lo[:, 0].rearrange("p e c i -> p (e c i)"),
                                  wg_st.rearrange("p e c i -> p (e c i)")),
                                 (wgu_hi[:, 1].rearrange("p e c i -> p (e c i)"),
                                  wgu_lo[:, 1].rearrange("p e c i -> p (e c i)"),
                                  wu_st.rearrange("p e c i -> p (e c i)")),
                                 (wd_hi[:, :, :], wd_lo[:, :, :], wd_st),
                                 (wr_hi[:, :, :], wr_lo[:, :, :], wr_sb[:, :, :])):
                v.tensor_tensor(lo, full, hi.bitcast(F32), ALU.subtract).then_inc(wlo_ready, 1)
            dve.wait_ge(iota_ready, 1)
            v.tensor_copy(iota_f[:, :], iota_u[:, :]).then_inc(iotaf_ready, 1)
            dve.wait_ge(iotaf_ready, 1)

            def body(st):
                c_on, y_on, r_on, b_on, m_on = st.on("C"), st.on("Y"), st.on("R"), st.on("B"), st.chain()
                if y_on:
                    q = st.slot("Y", 2)
                    dve.wait_ge(down_done, st.before("Y", EM, EM))
                    dve.wait_ge(conv_ready, st.before("Y", CT, CT))
                    for c in range(HC):
                        v.tensor_tensor(conv[:, q, c], ps_y[c][:, :], conv[:, q, c], ALU.add).then_inc(ysum_ready, 1)
                if c_on:
                    hidden(st, 0)
                if st.on("L"):
                    norm1_stats(st)
                for h in range(2):
                    if y_on:
                        k = st.slot("Y", 4)
                        dve.wait_ge(y_done, st.before("Y", 2, h + 1))
                        dve.wait_ge(relu_added, st.before("Y", 1, 1))
                        two = acc[:, k, 2 * h:2 * h + 2].rearrange("p t n -> p (t n)")
                        v.tensor_tensor(two, ps_sh[0][:, :], two, ALU.add).then_inc(out_ready, 1)
                    if h == 0:
                        if c_on:
                            hidden(st, 1)
                        if r_on:
                            q = st.slot("R", 2)
                            if st.later("R", 1):
                                dve.wait_ge(x2T_ready, st.before("R", HC))
                            if st.first("R"):
                                v.memset(x2T[:, q, :, 0:PAD], 0.0).then_inc(halo_ready, 1)
                            else:
                                v.tensor_copy(x2T[:, q, :, 0:PAD], x2T[:, 1 - q, :, GT:GT + PAD])\
                                    .then_inc(halo_ready, 1)
                        if c_on:
                            q = st.slot("C", 2)
                            dve.wait_ge(rt, st.before("C", RT, RT))
                            for t in range(TG):
                                a = acc[:, st.slot("C", 4), t]
                                v.scalar_tensor_tensor(a, x2[:, q, t], coef[:, q, t:t + 1], a, ALU.mult, ALU.add)\
                                    .then_inc(ident_added, 1)
                            dve.wait_ge(halo_ready, st.before("C", 1, 1))
                            conv_tap(st, 0)
                        if r_on:
                            dve.wait_ge(router_done, st.before("R", 1, 1))
                            v.tensor_copy(logits[:, :], ps_sh[0][:, 0:TG * NE]).then_inc(logits_ready, 1)
                if m_on:
                    dve.wait_ge(mhi_out, st.chains(1, 1))
                    v.tensor_tensor(m_lo[:, :, :], ps_sh[1][:, :].rearrange("p (c n) -> p c n", c=HC),
                                    m_hi[:, :, :].bitcast(F32), ALU.subtract).then_inc(mlo_out, 1)
                if st.on("L"):
                    norm1(st)
                if r_on:
                    route(st)
                if c_on:
                    hidden(st, 2)
                    conv_tap(st, 1)
                if b_on:
                    residual(st, 0)
                    norm2_stats(st, 0)
                if c_on:
                    conv_tap(st, 2)
                if b_on:
                    residual(st, 1)
                    norm2_stats(st, 1)
                if c_on:
                    hidden(st, 3)
                if b_on:
                    norm2(st)
                if st.on("A"):
                    for c in range(HC):
                        q = st.slot("A", 4)
                        dve.wait_ge(xnThi_ready, st.before("A", HC, c + 1))
                        v.tensor_tensor(xnT_lo[:, q, c], ps_sh[c][:, :], xnT_hi[:, q, c].bitcast(F32), ALU.subtract)\
                            .then_inc(xnTlo_ready, 1)

            steps(dve, body)

        @block.gpsimd
        def _(pool):
            g = nc.gpsimd
            g.memset(ident[:, :], 0.0).then_inc(zeroed, 1)
            pool.wait_ge(zeroed, 1)
            g.affine_select(out=ident[:, :], in_=ident[:, :], compare_op=ALU.not_equal, fill=1.0, base=0,
                            pattern=[[-1, P]], channel_multiplier=1).then_inc(ident_ready, 1)
            g.iota(iota_u[:, :], pattern=[[1, NE]], base=0, channel_multiplier=0).then_inc(iota_ready, 1)
            g.memset(half_neg[:, :], -0.5).then_inc(const_ready, 1)
            g.memset(inv_e[:, :], math.exp(-1.0)).then_inc(const_ready, 1)
            g.memset(eps_ln[:, :], EPS_LN).then_inc(const_ready, 1)
            pool.wait_ge(const_ready, 3)

            def inv_std(mv, out_sb, aggr, aggr_n, veps, veps_n, ready):
                pool.wait_ge(aggr, aggr_n)
                g.tensor_tensor(mv[:, :, 1], mv[:, :, 1], eps_ln[:, :], ALU.add).then_inc(veps, 1)
                pool.wait_ge(veps, veps_n)
                g.tensor_tensor(out_sb[:, :], mv[:, :, 1], half_neg[:, :], ALU.pow).then_inc(ready, 1)

            def gate_weight(st, e):
                q = st.slot("C", 2)
                if e == 0:
                    pool.wait_ge(cwb_loaded[q], st.uses("C", 2, 16, 16))
                pool.wait_ge(gate_ready, st.before("C", EM, e + 1))
                g.tensor_tensor(gate[:, e % 2], gate[:, e % 2], cwb[:, q, e], ALU.mult).then_inc(gatew_ready, 1)

            def hid_low(st, e):
                pool.wait_ge(hidhi_ready, st.before("C", EM, e + 1))
                if st.later("C", 1) or e > 1:
                    pool.wait_ge(down_done, st.before("C", EM, e - 1))
                g.tensor_tensor(hid_lo[:, e % 2], hid[:, e % 2], hid_hi[:, e % 2].bitcast(F32), ALU.subtract)\
                    .then_inc(hidlo_ready, 1)

            def x2T_low(st, c):
                q = st.slot("R", 2)
                pool.wait_ge(x2Thi_ready, st.before("R", HC, c + 1))
                g.tensor_tensor(x2T_lo[:, q, c], x2T[:, q, c, PAD:PAD + GT], x2T_hi[:, q, c].bitcast(F32),
                                ALU.subtract).then_inc(x2Tlo_ready, 1)

            def body(st):
                c_on, r_on = st.on("C"), st.on("R")
                if c_on:
                    gate_weight(st, 0)
                if r_on:
                    x2T_low(st, 0)
                if c_on:
                    hid_low(st, 0)
                if r_on:
                    x2T_low(st, 1)
                if c_on:
                    gate_weight(st, 1)
                    hid_low(st, 1)
                if st.on("L"):
                    inv_std(mv1, rstd1, aggr1, st.before("L", TG, TG), veps1, st.before("L", 1, 1), rstd1_ready)
                if r_on:
                    pool.wait_ge(logits_ready, st.before("R", 1, 1))
                    g.tensor_tensor(enx[:, :], inv_e[:, :], logits[:, :], ALU.pow).then_inc(enx_ready, 1)
                if c_on:
                    gate_weight(st, 2)
                if st.on("L"):
                    pool.wait_ge(xnhi_ready, st.before("L", 1, 1))
                    g.tensor_tensor(xn_lo[:, :, :], xn[:, st.slot("L", 2)], xn_hi[:, :, :].bitcast(F32),
                                    ALU.subtract).then_inc(xnlo_ready, 1)
                if c_on:
                    hid_low(st, 2)
                    pool.wait_ge(relu_ready, st.before("C", TG, TG))
                    k = st.slot("C", 4)
                    g.tensor_tensor(acc[:, k], acc[:, k], x2[:, st.slot("C", 2)], ALU.add).then_inc(relu_added, 1)
                    gate_weight(st, 3)
                if st.on("B"):
                    inv_std(mv2, rstd2, aggr2, st.before("B", TG, TG), veps2, st.before("B", 1, 1), rstd2_ready)
                if c_on:
                    hid_low(st, 3)

            steps(pool, body)


def kernel(**inputs):
    import numpy as np
    import concourse.bacc as bacc
    from concourse.bass_utils import run_bass_kernel_spmd as run

    nc = bacc.Bacc("TRN2", target_bir_lowering=False, num_devices=1)
    a = {k.split("_", 1)[1]: np.asarray(v) for k, v in inputs.items()}
    B, N, H = a["attn_x"].shape
    KC = a["ffn_conv_w"].shape[0]
    EM = a["ffn_Wg"].shape[0]
    laid_out = {
        "x": a["attn_x"].reshape(B * N, H),
        "wq": a["attn_wq"],
        "wkT": a["attn_wk"].T,
        "wvT": a["attn_wv"].T,
        "woT": a["attn_wo"].T,
        "wr": a["ffn_Wr"],
        "rbias": a["ffn_router_bias"],
        "wg": a["ffn_Wg"],
        "wu": a["ffn_Wu"],
        "wd": a["ffn_Wd"],
        "convwb": np.concatenate([a["ffn_conv_w"].reshape(KC, H).T, a["ffn_conv_b"].reshape(H, 1)], axis=1),
    }
    arrays, args = {}, []
    for name, v in laid_out.items():
        v = np.ascontiguousarray(v)
        arrays[f"in_{name}"] = v
        args.append(nc.dram_tensor(f"in_{name}", v.shape, mybir.dt.from_np(v.dtype), kind="ExternalInput").ap())
    group = 4 * P
    args.append(nc.dram_tensor("cw_rows", (B * N // group, EM, group), F32, kind="Internal").ap())
    args.append(nc.dram_tensor("out_0", (B * N, H), F32, kind="ExternalOutput").ap())
    program(nc, *args)
    r = run(nc, [arrays], core_ids=[0])
    return r.results[0]["out_0"].reshape(B, N, H)
```

```python
import math
from contextlib import ExitStack

import concourse.bass as bass
from concourse import mybir

F32 = mybir.dt.float32
F32R = mybir.dt.float32r
U32 = mybir.dt.uint32
ALU = mybir.AluOpType
ACT = mybir.ActivationFunctionType
AXX = mybir.AxisListType.X

P = 128
LAG = {"L": 0, "A": 1, "X": 4, "B": 5, "R": 6, "C": 7, "Y": 8}
UNROLL = 4
EPS_LN = 1e-5
EPS_W = 1e-9


class Step:

    def __init__(self, r, s, groups):
        self.r, self.s, self.groups = r, s, groups
        self.peeled = isinstance(r, int)

    def on(self, stage):
        return not self.peeled or 0 <= UNROLL * self.r + self.s - LAG[stage] < self.groups

    def was_on(self, stage):
        return not self.peeled or 0 <= UNROLL * self.r + self.s - 1 - LAG[stage] < self.groups

    def later(self, stage, n):
        return not self.peeled or UNROLL * self.r + self.s - LAG[stage] >= n

    def first(self, stage):
        return (self.s - LAG[stage]) % UNROLL == 0

    def last(self, stage):
        return (self.s - LAG[stage]) % UNROLL == UNROLL - 1

    def group(self, stage):
        return UNROLL * self.r + (self.s - LAG[stage])

    def slot(self, stage, n):
        return (self.s - LAG[stage]) % n

    def before(self, stage, per=1, extra=0):
        n = self.s - LAG[stage]
        if self.peeled:
            return per * min(max(UNROLL * self.r + n, 0), self.groups) + extra
        return self.r * (UNROLL * per) + (n * per + extra)

    def uses(self, stage, n, per=1, extra=0):
        k = (self.s - LAG[stage]) // n
        return self.r * (UNROLL // n * per) + (k * per + extra)

    def chains(self, per=1, extra=0):
        k = (self.s - LAG["B"] - 1) // UNROLL + 1
        if self.peeled:
            return per * min(max(self.r + k, 0), self.groups // UNROLL) + extra
        return self.r * per + (k * per + extra)

    def chain(self):
        return self.first("B") and self.on("B")


GU_BANK = [k % 3 for k in range(8)]


def program(nc, x, wq, wkT, wvT, woT, wr, rbias, wg, wu, wd, convwb, cw_rows, out):
    T, H = x.shape
    D = wq.shape[0]
    NE = wr.shape[1]
    EM, _, I = wg.shape
    KC = convwb.shape[1] - 1
    HC = H // P
    TG = 4
    GT = TG * P
    NG = T // GT
    SCALE = math.sqrt(3.0 / D)
    assert D == 64 and I == P and HC == 2 and NG % UNROLL == 0
    ROUNDS = (NG + max(LAG.values())) // UNROLL
    LOOP = (LAG["Y"] // UNROLL, NG // UNROLL)

    x_rows = x.rearrange("(n p) f -> p n f", p=P)
    out_rows = out.rearrange("(n p) f -> p n f", p=P)

    ctx = ExitStack()
    with ctx:
        def sb(name, shape, dt=F32):
            return ctx.enter_context(nc.sbuf_tensor(name, shape, dt))

        def bank(name):
            return ctx.enter_context(nc.psum_tensor(name, [P, 512], F32))

        def sem(name):
            return ctx.enter_context(nc.semaphore(name))

        wq_sb = sb("wq_sb", [D, H])
        wkT_sb = sb("wkT_sb", [P, HC, D])
        wvT_sb = sb("wvT_sb", [P, HC, D])
        woT_sb = sb("woT_sb", [D, H])
        wr_sb = sb("wr_sb", [P, HC, NE])
        wgu_hi = sb("wgu_hi", [P, 2, EM, HC, I], F32R)
        wgu_lo = sb("wgu_lo", [P, 2, EM, HC, I], F32R)
        wd_hi = sb("wd_hi", [P, EM, H], F32R)
        wd_lo = sb("wd_lo", [P, EM, H], F32R)
        conv_w = sb("conv_w", [P, HC, KC + 1])
        bias8 = sb("bias8", [P, NE])
        ident = sb("ident", [P, P])
        ident_r = sb("ident_r", [P, P], F32R)
        iota_u = sb("iota_u", [P, NE], U32)
        iota_f = sb("iota_f", [P, NE])
        tick = sb("tick", [1, 1])
        eps_ln = sb("eps_ln", [P, TG])
        zero4 = sb("zero4", [P, TG])
        half_neg = sb("half_neg", [P, TG])
        inv_e = sb("inv_e", [P, TG * NE])

        xa = sb("xa", [P, 2, TG, H])
        stats1 = sb("stats1", [P, TG, 6])
        mv1 = sb("mv1", [P, TG, 2])
        negm1 = sb("negm1", [P, TG])
        rstd1 = sb("rstd1", [P, TG])
        shift1 = sb("shift1", [P, TG])
        xn = sb("xn", [P, TG, H])
        xn_hi = sb("xn_hi", [P, 2, TG, H], F32R)
        xn_lo = sb("xn_lo", [P, 2, TG, H], F32R)
        xnT_hi = sb("xnT_hi", [P, 4, HC, GT], F32R)
        xnT_lo = sb("xnT_lo", [P, 4, HC, GT], F32R)
        gram = sb("gram", [P, HC, H])
        p1 = sb("p1", [P, HC, D])
        et = sb("et", [D, D])
        ff = sb("ff", [D, H])
        m_hi = sb("m_hi", [P, HC, H], F32R)
        m_lo = sb("m_lo", [P, HC, H], F32R)
        acc = sb("acc", [P, 4, TG, H])
        stats2 = sb("stats2", [P, TG, 6])
        mv2 = sb("mv2", [P, TG, 2])
        negm2 = sb("negm2", [P, TG])
        rstd2 = sb("rstd2", [P, TG])
        shift2 = sb("shift2", [P, TG])
        x2 = sb("x2", [P, 2, TG, H])
        PAD = KC - 1
        x2T = sb("x2T", [P, 2, HC, PAD + GT])
        x2T_hi = sb("x2T_hi", [P, 2, HC, GT], F32R)
        x2T_lo = sb("x2T_lo", [P, 2, HC, GT], F32R)
        logits = sb("logits", [P, TG * NE])
        enx = sb("enx", [P, TG * NE])
        den = sb("den", [P, TG * NE])
        score = sb("score", [P, TG, NE])
        biased = sb("biased", [P, TG, NE])
        top8 = sb("top8", [P, TG, 8])
        idx8 = sb("idx8", [P, TG, 8], U32)
        idxf = sb("idxf", [P, TG, 2])
        hot = sb("hot", [P, 2, TG, NE])
        chosen = sb("chosen", [P, TG, NE])
        raw = sb("raw", [P, TG, NE])
        wsum = sb("wsum", [P, TG])
        wsum_eps = sb("wsum_eps", [P, TG])
        winv = sb("winv", [P, TG])
        cw = sb("cw", [P, 2, TG, NE])
        coef = sb("coef", [P, 2, TG])
        cwT = sb("cwT", [EM, GT])
        cwb = sb("cwb", [P, 2, EM, GT])
        gate = sb("gate", [P, 2, GT])
        hid = sb("hid", [P, 2, GT])
        hid_hi = sb("hid_hi", [P, 2, GT], F32R)
        hid_lo = sb("hid_lo", [P, 2, GT], F32R)
        conv = sb("conv", [P, 2, HC, GT])
        w_stage = cwb[:, :, :, :].rearrange("p a e n -> p (a e n)")
        wg_st = w_stage[:, 0:EM * HC * I].rearrange("p (e c i) -> p e c i", e=EM, c=HC)
        wu_st = w_stage[:, EM * HC * I:2 * EM * HC * I].rearrange("p (e c i) -> p e c i", e=EM, c=HC)
        wd_st = w_stage[:, 2 * EM * HC * I:2 * EM * HC * I + EM * H].rearrange("p (e n) -> p e n", e=EM)

        ps_gram = bank("ps_gram")
        ps_gu = [bank(f"ps_gu{k}") for k in range(3)]
        ps_y = [bank(f"ps_y{h}") for h in range(2)]
        ps_sh = [bank(f"ps_sh{k}") for k in range(2)]

        w_loaded = sem("w_loaded")
        xa_loaded = [sem(f"xa_loaded{k}") for k in range(2)]
        acc_loaded = [sem(f"acc_loaded{k}") for k in range(4)]
        out_stored = [sem(f"out_stored{k}") for k in range(4)]
        cw_stored = sem("cw_stored")
        cwb_loaded = [sem(f"cwb_loaded{k}") for k in range(2)]
        zeroed = sem("zeroed")
        ident_ready = sem("ident_ready")
        identr_ready = sem("identr_ready")
        const_ready = sem("const_ready")
        iota_ready = sem("iota_ready")
        iotaf_ready = sem("iotaf_ready")
        whi_ready = sem("whi_ready")
        wlo_ready = sem("wlo_ready")
        stat1 = sem("stat1")
        aggr1 = sem("aggr1")
        veps1 = sem("veps1")
        rstd1_ready = sem("rstd1_ready")
        shift1_ready = sem("shift1_ready")
        xn_ready = sem("xn_ready")
        xnhi_ready = sem("xnhi_ready")
        xnlo_ready = sem("xnlo_ready")
        gram_done = sem("gram_done")
        gram_out = sem("gram_out")
        gramT_done, gramT_out = sem("gramT_done"), sem("gramT_out")
        p1_done, p1_out = sem("p1_done"), sem("p1_out")
        et_done, et_out = sem("et_done"), sem("et_out")
        f_done, f_out = sem("f_done"), sem("f_out")
        m_done, mhi_out, mlo_out = sem("m_done"), sem("mhi_out"), sem("mlo_out")
        xnT_done = sem("xnT_done")
        xnT_out = sem("xnT_out")
        attn_done = sem("attn_done")
        x1_ready = sem("x1_ready")
        stat2 = sem("stat2")
        aggr2 = sem("aggr2")
        veps2 = sem("veps2")
        rstd2_ready = sem("rstd2_ready")
        shift2_ready = sem("shift2_ready")
        x2_ready = sem("x2_ready")
        x2T_done = sem("x2T_done")
        x2T_ready = sem("x2T_ready")
        x2Thi_ready = sem("x2Thi_ready")
        x2Tlo_ready = sem("x2Tlo_ready")
        halo_ready = sem("halo_ready")
        router_done = sem("router_done")
        logits_ready = sem("logits_ready")
        enx_ready = sem("enx_ready")
        rt = sem("rt")
        cw_ready = sem("cw_ready")
        cwT_done = sem("cwT_done")
        cwT_ready = sem("cwT_ready")
        gu_done = sem("gu_done")
        gate_ready = sem("gate_ready")
        gatew_ready = sem("gatew_ready")
        hid_ready = sem("hid_ready")
        hidhi_ready = sem("hidhi_ready")
        hidlo_ready = [sem(f"hidlo_ready{k}") for k in range(2)]
        down_done = sem("down_done")
        tap_ready = sem("tap_ready")
        conv_ready = sem("conv_ready")
        ident_added = sem("ident_added")
        relu_ready = sem("relu_ready")
        relu_added = sem("relu_added")
        y_done = sem("y_done")
        out_ready = sem("out_ready")

        CT = HC * PAD
        XT = 2 * HC
        N_LOADS = 7 + 2 * EM + 1
        NSPLIT = 3

        def steps(eng, body):
            for r in range(LOOP[0]):
                for s in range(UNROLL):
                    body(Step(r, s, NG))
            with eng.Fori(LOOP[0], LOOP[1], 1) as r:
                for s in range(UNROLL):
                    body(Step(r, s, NG))
            for r in range(LOOP[1], ROUNDS):
                for s in range(UNROLL):
                    body(Step(r, s, NG))

        block = ctx.enter_context(nc.Block())

        @block.sync
        def _(sp):
            def load_x(st):
                if st.later("L", 2):
                    sp.wait_ge(xn_ready, st.before("L", TG, -TG))
                sp.dma_start(xa[:, st.slot("L", 2)], x_rows[:, bass.ds(st.group("L") * TG, TG), :])\
                    .then_inc(xa_loaded[st.slot("L", 2)], 16)

            load_x(Step(0, 0, NG))
            load_x(Step(0, 1, NG))
            sp.dma_start(wq_sb[:, :], wq).then_inc(w_loaded, 16)
            sp.dma_start(wkT_sb[:, :, :], wkT.rearrange("(c p) d -> p c d", p=P)).then_inc(w_loaded, 16)
            sp.dma_start(wvT_sb[:, :, :], wvT.rearrange("(c p) d -> p c d", p=P)).then_inc(w_loaded, 16)
            sp.dma_start(woT_sb[:, :], woT).then_inc(w_loaded, 16)
            sp.dma_start(wr_sb[:, :, :], wr.rearrange("(c p) e -> p c e", p=P)).then_inc(w_loaded, 16)
            sp.dma_start(conv_w[:, :, :], convwb.rearrange("(c p) k -> p c k", p=P)).then_inc(w_loaded, 16)
            sp.dma_start(bias8[:, :], rbias.partition_broadcast(P)).then_inc(w_loaded, 16)
            for e in range(EM):
                sp.dma_start(wg_st[:, e], wg[e].rearrange("(c p) i -> p c i", p=P)).then_inc(w_loaded, 16)
                sp.dma_start(wu_st[:, e], wu[e].rearrange("(c p) i -> p c i", p=P)).then_inc(w_loaded, 16)
            sp.dma_start(wd_st, wd.rearrange("e i n -> i e n")).then_inc(w_loaded, 16)

            def body(st):
                if st.on("L") and not (st.peeled and st.group("L") < 2):
                    load_x(st)
                if st.on("Y"):
                    k = st.slot("Y", 4)
                    for h in range(2):
                        sp.wait_ge(out_ready, st.before("Y", 2, h + 1))
                        sp.dma_start(out_rows[:, bass.ds(st.group("Y") * TG + 2 * h, 2), :],
                                     acc[:, k, 2 * h:2 * h + 2]).then_inc(out_stored[k], 16)
                if st.on("R"):
                    k = st.slot("R", 2)
                    rows = cw_rows[bass.ds(st.group("R"), 1)]
                    sp.wait_ge(cwT_ready, st.before("R", 1, 1))
                    sp.dma_start(rows.rearrange("a e n -> (a e) n"), cwT[:, :]).then_inc(cw_stored, 16)
                    sp.wait_ge(cw_stored, st.before("R", 16, 16))
                    if st.peeled and st.before("R") < 2:
                        sp.wait_ge(whi_ready, NSPLIT)
                        sp.wait_ge(wlo_ready, NSPLIT)
                    sp.dma_start(cwb[:, k].rearrange("p e n -> p (e n)"),
                                 rows.rearrange("a e n -> (a e n)").partition_broadcast(P))\
                        .then_inc(cwb_loaded[k], 16)
                if st.on("X"):
                    k = st.slot("X", 4)
                    if st.later("X", 4):
                        sp.wait_ge(out_stored[k], st.uses("X", 4, 32))
                    sp.dma_start(acc[:, k], x_rows[:, bass.ds(st.group("X") * TG, TG), :])\
                        .then_inc(acc_loaded[k], 16)

            steps(sp, body)
            for k in range(4):
                sp.wait_ge(out_stored[k], 32 * (NG // 4))
            sp.wait_ge(cw_stored, 16 * NG)

        @block.tensor
        def _(pe):
            def three(dst, a_hi, a_lo, b_hi, b_lo, start, stop):
                nc.tensor.matmul(dst, a_hi, b_hi, start=start, stop=False, skip_group_check=True)
                nc.tensor.matmul(dst, a_hi, b_lo, start=False, stop=False, skip_group_check=True)
                return nc.tensor.matmul(dst, a_lo, b_hi, start=False, stop=stop, skip_group_check=True)

            def gate_up(st, k):
                e, w = divmod(k, 2)
                q = st.slot("C", 2)
                if k == 0:
                    pe.wait_ge(x2Tlo_ready, st.before("C", HC, HC))
                if k >= 3:
                    ke, kw = divmod(k - 3, 2)
                    pe.wait_ge((gate_ready, hid_ready)[kw], st.before("C", EM, ke + 1))
                else:
                    ke, kw = divmod((6, 7, 5)[k], 2)
                    if st.later("C", 1):
                        pe.wait_ge((gate_ready, hid_ready)[kw], st.before("C", EM, ke + 1 - EM))
                for c in range(HC):
                    last = three(ps_gu[GU_BANK[k]][:, :], wgu_hi[:, w, e, c], wgu_lo[:, w, e, c],
                                 x2T_hi[:, q, c], x2T_lo[:, q, c], c == 0, c == HC - 1)
                last.then_inc(gu_done, 1)

            def down(st, stage, e):
                pe.wait_ge(hidlo_ready[e % 2], st.before(stage, EM // 2, e // 2 + 1))
                if e == 0 and st.later(stage, 1):
                    pe.wait_ge(out_ready, st.before(stage, 2))
                q = e % 2
                for h in range(2):
                    for k in range(2):
                        tok = slice((2 * h + k) * P, (2 * h + k + 1) * P)
                        last = three(ps_y[h][:, k * H:(k + 1) * H], hid_hi[:, q, tok], hid_lo[:, q, tok],
                                     wd_hi[:, e], wd_lo[:, e], e == 0 and k == 0, False)
                last.then_inc(down_done, 1)

            def conv_add(st):
                q = st.slot("Y", 2)
                pe.wait_ge(conv_ready, st.before("Y", CT, CT))
                for h in range(2):
                    for k in range(2):
                        t = 2 * h + k
                        for c in range(HC):
                            at = k * H + c * P
                            last = nc.tensor.matmul(ps_y[h][:, at:at + P], conv[:, q, c, t * P:(t + 1) * P],
                                                    ident[:, :], start=False, stop=True, skip_group_check=True)
                    last.then_inc(y_done, 1)

            def gram_matrix(st):
                pe.wait_ge(xnlo_ready, st.before("A", 1, 1))
                if st.first("A") and st.chain():
                    pe.wait_ge(gram_out, st.chains(2, 2))
                q = st.slot("A", 2)
                for t in range(TG):
                    start = st.first("A") and t == 0
                    stop = st.last("A") and t == TG - 1
                    three(ps_gram[:, 0:H], xn_hi[:, q, t, 0:P], xn_lo[:, q, t, 0:P],
                          xn_hi[:, q, t, :], xn_lo[:, q, t, :], start, stop)
                    last = three(ps_gram[:, H:H + P], xn_hi[:, q, t, P:H], xn_lo[:, q, t, P:H],
                                 xn_hi[:, q, t, P:H], xn_lo[:, q, t, P:H], False, stop)
                last.then_inc(gram_done, 1)

            def xn_transpose(st, part):
                src, q = (xn_hi, xn_lo)[part], st.slot("A", 2)
                for c in range(HC):
                    if part == 1:
                        pe.wait_ge(xnT_out, st.before("A", XT, c + 1))
                    elif c == 1 and st.on("R"):
                        pe.wait_ge(cwT_ready, st.before("R", 1, 1))
                    elif st.on("B"):
                        pe.wait_ge(x1_ready, st.before("B", 2, 2 - c))
                    elif st.later("A", 1):
                        pe.wait_ge(xnT_out, st.before("A", XT, c - 1))
                    for t in range(TG):
                        last = nc.tensor.matmul(ps_sh[c][:, t * P:(t + 1) * P], src[:, q, t, c * P:(c + 1) * P],
                                                ident_r[:, :], start=True, stop=True)
                    last.then_inc(xnT_done, 1)

            def x2_transpose(st, c):
                if c == 0:
                    pe.wait_ge(x2_ready, st.before("R", TG, TG))
                if st.was_on("A"):
                    pe.wait_ge(xnT_out, st.before("A", XT, c - 1))
                elif c == 0:
                    pe.wait_ge(x1_ready, st.before("B", 2))
                else:
                    pe.wait_ge(cwT_ready, st.before("R"))
                for t in range(TG):
                    last = nc.tensor.transpose(ps_sh[c][:, t * P:(t + 1) * P],
                                               x2[:, st.slot("R", 2), t, c * P:(c + 1) * P], ident[:, :])
                last.then_inc(x2T_done, 1)

            def router(st):
                pe.wait_ge(x2T_ready, st.before("R", HC, HC))
                pe.wait_ge(x2Tlo_ready, st.before("R", HC, 1))
                b, q = ps_sh[0], st.slot("R", 2)
                for t in range(TG):
                    for c in range(HC):
                        last = nc.tensor.matmul(b[:, t * NE:(t + 1) * NE],
                                                x2T[:, q, c, PAD + t * P:PAD + (t + 1) * P], wr_sb[:, c],
                                                start=(c == 0), stop=(c == HC - 1))
                last.then_inc(router_done, 1)

            def attention(st, h):
                if h == 0 and st.chain():
                    pe.wait_ge(mlo_out, st.chains(1, 1))
                elif h == 0:
                    pe.wait_ge(x2Tlo_ready, st.before("R", HC, HC))
                elif st.on("R"):
                    pe.wait_ge(logits_ready, st.before("R", 1, 1))
                else:
                    pe.wait_ge(xnT_out, st.before("A", XT, -1))
                if h == 0:
                    pe.wait_ge(xnT_out, st.before("B", XT, XT))
                b, q = ps_sh[1 - h], st.slot("B", 4)
                for k in range(2):
                    tok = slice((2 * h + k) * P, (2 * h + k + 1) * P)
                    for c in range(HC):
                        last = three(b[:, k * H:(k + 1) * H], xnT_hi[:, q, c, tok], xnT_lo[:, q, c, tok],
                                     m_hi[:, c], m_lo[:, c], c == 0, c == HC - 1)
                last.then_inc(attn_done, 1)

            def weights_transpose(st):
                pe.wait_ge(cw_ready, st.before("R", 1, 1))
                if st.on("B"):
                    pe.wait_ge(x1_ready, st.before("B", 2, 1))
                else:
                    pe.wait_ge(x2Tlo_ready, st.before("R", HC, HC))
                b = ps_sh[1]
                for t in range(TG):
                    last = nc.tensor.transpose(b[0:EM, t * P:(t + 1) * P], cw[:, st.slot("R", 2), t, 0:EM],
                                               ident[:, :])
                last.then_inc(cwT_done, 1)

            def chain_gramT(st):
                pe.wait_ge(gram_out, st.chains(2, 2))
                if st.on("R"):
                    pe.wait_ge(x2Tlo_ready, st.before("R", HC, HC))
                else:
                    pe.wait_ge(xnT_out, st.before("A", XT))
                b = ps_sh[1]
                nc.tensor.transpose(b[:, 0:P], gram[:, 0, P:H], ident[:, :]).then_inc(gramT_done, 1)

            def chain_p1(st):
                pe.wait_ge(gramT_out, st.chains(1, 1))
                b = ps_sh[1]
                for m in range(HC):
                    for c in range(HC):
                        last = nc.tensor.matmul(b[:, m * D:(m + 1) * D], gram[:, c, m * P:(m + 1) * P], wvT_sb[:, c],
                                                start=(c == 0), stop=(c == HC - 1))
                last.then_inc(p1_done, 1)

            def chain_et(st):
                pe.wait_ge(p1_out, st.chains(1, 1))
                b = ps_sh[1]
                for c in range(HC):
                    last = nc.tensor.matmul(b[0:D, 0:D], p1[:, c], wkT_sb[:, c], start=(c == 0), stop=(c == HC - 1))
                last.then_inc(et_done, 1)

            def chain_f(st):
                b = ps_sh[1]
                nc.tensor.matmul(b[0:D, 0:H], et[:, :], woT_sb[:, :], start=True, stop=True).then_inc(f_done, 1)

            def chain_m(st):
                pe.wait_ge(f_out, st.chains(1, 1))
                b = ps_sh[1]
                for c in range(HC):
                    last = nc.tensor.matmul(b[:, c * H:(c + 1) * H], wq_sb[:, c * P:(c + 1) * P], ff[:, :],
                                            start=True, stop=True)
                last.then_inc(m_done, 1)

            pe.wait_ge(identr_ready, 1)

            def body(st):
                c_on, y_on, r_on, a_on, b_on, m_on = (st.on("C"), st.on("Y"), st.on("R"), st.on("A"), st.on("B"),
                                                      st.chain())
                if st.peeled and b_on and st.before("B") == 0:
                    pe.wait_ge(w_loaded, 16 * N_LOADS)
                if st.peeled and c_on and st.before("C") == 0:
                    pe.wait_ge(wlo_ready, NSPLIT)
                if r_on:
                    x2_transpose(st, 0)
                if c_on:
                    gate_up(st, 0)
                if r_on:
                    x2_transpose(st, 1)
                if c_on:
                    gate_up(st, 1)
                if m_on:
                    chain_gramT(st)
                if y_on:
                    down(st, "Y", EM - 1)
                if m_on:
                    chain_p1(st)
                if r_on:
                    router(st)
                if c_on:
                    gate_up(st, 2)
                if m_on:
                    chain_et(st)
                if y_on:
                    conv_add(st)
                if m_on:
                    pe.wait_ge(et_out, st.chains(1, 1))
                if c_on:
                    gate_up(st, 3)
                if m_on:
                    chain_f(st)
                if c_on:
                    gate_up(st, 4)
                if m_on:
                    chain_m(st)
                if c_on:
                    down(st, "C", 0)
                if b_on:
                    attention(st, 0)
                if c_on:
                    gate_up(st, 5)
                if b_on:
                    attention(st, 1)
                if c_on:
                    down(st, "C", 1)
                    gate_up(st, 6)
                    gate_up(st, 7)
                if a_on:
                    gram_matrix(st)
                if r_on:
                    weights_transpose(st)
                if a_on:
                    xn_transpose(st, 0)
                if c_on:
                    down(st, "C", 2)
                if a_on:
                    xn_transpose(st, 1)

            steps(pe, body)

        @block.scalar
        def _(act):
            def copy(dst, src, scale=1.0):
                return nc.scalar.activation(dst, src, ACT.Copy, scale=scale)

            def silu(st, e):
                act.wait_ge(gu_done, st.before("C", 2 * EM, 2 * e + 1))
                if st.later("C", 1) or e > 1:
                    act.wait_ge(hid_ready, st.before("C", EM, e - 1))
                nc.scalar.activation(gate[:, e % 2], ps_gu[GU_BANK[2 * e]][:, :], ACT.Silu)\
                    .then_inc(gate_ready, 1)

            def hid_high(st, e):
                act.wait_ge(hid_ready, st.before("C", EM, e + 1))
                if st.later("C", 1) or e > 1:
                    act.wait_ge(down_done, st.before("C", EM, e - 1))
                copy(hid_hi[:, e % 2], hid[:, e % 2]).then_inc(hidhi_ready, 1)

            def x2T_out(st, c):
                act.wait_ge(x2T_done, st.before("R", HC, c + 1))
                q = st.slot("R", 2)
                if c == 0:
                    if st.later("R", 2):
                        act.wait_ge(conv_ready, st.before("R", CT, -CT))
                    if st.later("R", 1):
                        act.wait_ge(halo_ready, st.before("R"))
                    if st.later("R", 2):
                        act.wait_ge(gu_done, st.before("R", 2 * EM, -2 * EM))
                copy(x2T[:, q, c, PAD:PAD + GT], ps_sh[c][:, :]).then_inc(x2T_ready, 1)
                copy(x2T_hi[:, q, c], ps_sh[c][:, :]).then_inc(x2Thi_ready, 1)

            def chain_copy(st, done, count, pairs, out_sem, scale=1.0):
                act.wait_ge(done, count)
                for dst, src in pairs:
                    copy(dst, src, scale).then_inc(out_sem, 1)

            act.wait_ge(ident_ready, 1)
            copy(ident_r[:, :], ident[:, :]).then_inc(identr_ready, 1)

            def split_weights():
                act.wait_ge(w_loaded, 16 * N_LOADS)
                copy(wgu_hi[:, 0].rearrange("p e c i -> p (e c i)"), wg_st.rearrange("p e c i -> p (e c i)"))\
                    .then_inc(whi_ready, 1)
                copy(wgu_hi[:, 1].rearrange("p e c i -> p (e c i)"), wu_st.rearrange("p e c i -> p (e c i)"))\
                    .then_inc(whi_ready, 1)
                copy(wd_hi[:, :, :], wd_st).then_inc(whi_ready, 1)

            def norm1(st):
                q = st.slot("L", 2)
                act.wait_ge(shift1_ready, st.before("L", 1, 1))
                if st.later("L", 1):
                    act.wait_ge(xnlo_ready, st.before("L"))
                for t in range(TG):
                    nc.scalar.activation(xn[:, t], xa[:, q, t], ACT.Identity, bias=shift1[:, t:t + 1],
                                         scale=rstd1[:, t:t + 1]).then_inc(xn_ready, 1)

            def norm2(st):
                q = st.slot("B", 2)
                act.wait_ge(shift2_ready, st.before("B", 1, 1))
                if st.later("B", 2):
                    act.wait_ge(relu_added, st.before("B", 1, -1))
                if st.later("B", 2):
                    act.wait_ge(x2T_done, st.before("B", HC, -HC))
                for t in range(TG):
                    nc.scalar.activation(x2[:, q, t], acc[:, st.slot("B", 4), t], ACT.Identity,
                                         bias=shift2[:, t:t + 1], scale=rstd2[:, t:t + 1]).then_inc(x2_ready, 1)

            def xnT_copy(st, part):
                q = st.slot("A", 4)
                for c in range(HC):
                    act.wait_ge(xnT_done, st.before("A", XT, part * HC + c + 1))
                    copy((xnT_hi, xnT_lo)[part][:, q, c], ps_sh[c][:, :]).then_inc(xnT_out, 1)

            def body(st):
                c_on, r_on, m_on, a_on = st.on("C"), st.on("R"), st.chain(), st.on("A")
                if st.peeled and st.r == 0 and st.s == 2:
                    split_weights()
                if m_on:
                    chain_copy(st, gram_done, st.before("A"),
                               [(gram[:, 0, :], ps_gram[:, 0:H]), (gram[:, 1, P:H], ps_gram[:, H:H + P])], gram_out)
                if r_on:
                    x2T_out(st, 0)
                if c_on:
                    silu(st, 0)
                    q = st.slot("C", 2)
                    act.wait_ge(x2T_ready, st.before("C", HC, HC))
                    if st.later("C", 2):
                        act.wait_ge(y_done, st.before("C", 2, -2))
                    for c in range(HC):
                        nc.scalar.activation(conv[:, q, c], x2T[:, q, c, PAD:PAD + GT], ACT.Identity,
                                             bias=conv_w[:, c, KC:KC + 1], scale=conv_w[:, c, PAD:PAD + 1])\
                            .then_inc(tap_ready, 1)
                if r_on:
                    x2T_out(st, 1)
                if m_on:
                    chain_copy(st, gramT_done, st.chains(1, 1), [(gram[:, 1, 0:P], ps_sh[1][:, 0:P])], gramT_out)
                if c_on:
                    hid_high(st, 0)
                if m_on:
                    chain_copy(st, p1_done, st.chains(1, 1),
                               [(p1[:, :, :], ps_sh[1][:, 0:HC * D].rearrange("p (c d) -> p c d", c=HC))], p1_out)
                if c_on:
                    silu(st, 1)
                if m_on:
                    chain_copy(st, et_done, st.chains(1, 1), [(et[:, :], ps_sh[1][0:D, 0:D])], et_out)
                if c_on:
                    q = st.slot("C", 2)
                    for t in range(TG):
                        act.wait_ge(ident_added, st.before("C", TG, t + 1))
                        nc.scalar.activation(x2[:, q, t], x2[:, q, t], ACT.Relu, scale=cw[:, q, t, EM + 3:EM + 4])\
                            .then_inc(relu_ready, 1)
                if m_on:
                    chain_copy(st, f_done, st.chains(1, 1), [(ff[:, :], ps_sh[1][0:D, 0:H])], f_out, SCALE)
                if c_on:
                    silu(st, 2)
                if m_on:
                    chain_copy(st, m_done, st.chains(1, 1),
                               [(m_hi[:, :, :], ps_sh[1][:, :].rearrange("p (c n) -> p c n", c=HC))], mhi_out)
                if c_on:
                    hid_high(st, 1)
                if st.on("L"):
                    norm1(st)
                if st.on("B"):
                    norm2(st)
                if c_on:
                    hid_high(st, 2)
                    silu(st, 3)
                if st.on("L"):
                    act.wait_ge(xn_ready, st.before("L", TG, TG))
                    if st.later("L", 2):
                        act.wait_ge(xnT_done, st.before("L", XT, -XT))
                    copy(xn_hi[:, st.slot("L", 2)], xn[:, :, :]).then_inc(xnhi_ready, 1)
                if r_on:
                    act.wait_ge(cwT_done, st.before("R", 1, 1))
                    if st.later("R", 1):
                        act.wait_ge(cw_stored, st.before("R", 16))
                    copy(cwT[:, :], ps_sh[1][0:EM, :]).then_inc(cwT_ready, 1)
                if a_on:
                    xnT_copy(st, 0)
                if c_on:
                    hid_high(st, 3)
                if a_on:
                    xnT_copy(st, 1)

            steps(act, body)

        @block.vector
        def _(dve):
            v = nc.vector

            def turn(sem, count):
                dve.wait_ge(sem, count)
                v.tensor_copy(tick[:, :], iota_f[0:1, 0:1])

            def hidden(st, e):
                dve.wait_ge(gatew_ready, st.before("C", EM, e + 1))
                dve.wait_ge(gu_done, st.before("C", 2 * EM, 2 * e + 2))
                if st.later("C", 1) or e > 1:
                    dve.wait_ge(hidlo_ready[e % 2], st.before("C", EM // 2, e // 2))
                v.tensor_tensor(hid[:, e % 2], ps_gu[GU_BANK[2 * e + 1]][:, :], gate[:, e % 2], ALU.mult)\
                    .then_inc(hid_ready, 1)

            def hid_low(st, e):
                dve.wait_ge(hidhi_ready, st.before("C", EM, e + 1))
                v.tensor_tensor(hid_lo[:, 0], hid[:, 0], hid_hi[:, 0].bitcast(F32), ALU.subtract)\
                    .then_inc(hidlo_ready[0], 1)

            def conv_tap(st, n):
                q, k = st.slot("C", 2), PAD - 1 - n
                for c in range(HC):
                    if n == 0:
                        dve.wait_ge(tap_ready, st.before("C", HC, c + 1))
                    else:
                        dve.wait_ge(conv_ready, st.before("C", CT, HC * (n - 1) + c + 1))
                    v.scalar_tensor_tensor(conv[:, q, c], x2T[:, q, c, k:k + GT], conv_w[:, c, k:k + 1],
                                           conv[:, q, c], ALU.mult, ALU.add).then_inc(conv_ready, 1)

            def norm1_stats(st):
                q = st.slot("L", 2)
                dve.wait_ge(xa_loaded[q], st.uses("L", 2, 16, 16))
                if st.later("L", 1):
                    dve.wait_ge(shift1_ready, st.before("L"))
                for t in range(TG):
                    v.bn_stats(stats1[:, t], xa[:, q, t]).then_inc(stat1, 1)
                turn(stat1, st.before("L", TG, TG))
                for t in range(TG):
                    v.bn_aggr(mv1[:, t], stats1[:, t]).then_inc(aggr1, 1)

            def residual(st, h):
                q = st.slot("B", 4)
                dve.wait_ge(attn_done, st.before("B", 2, h + 1))
                if h == 0:
                    dve.wait_ge(acc_loaded[q], st.uses("B", 4, 16, 16))
                two = acc[:, q, 2 * h:2 * h + 2].rearrange("p t n -> p (t n)")
                v.tensor_tensor(two, ps_sh[1 - h][:, :], two, ALU.add).then_inc(x1_ready, 1)

            def norm2_stats(st, h):
                q = st.slot("B", 4)
                dve.wait_ge(x1_ready, st.before("B", 2, h + 1))
                if h == 0 and st.later("B", 1):
                    dve.wait_ge(shift2_ready, st.before("B"))
                for t in (2 * h, 2 * h + 1):
                    v.bn_stats(stats2[:, t], acc[:, q, t]).then_inc(stat2, 1)
                turn(stat2, st.before("B", TG, 2 * h + 2))
                for t in (2 * h, 2 * h + 1):
                    v.bn_aggr(mv2[:, t], stats2[:, t]).then_inc(aggr2, 1)

            RT = 12 + 2 * TG

            def flat(t):
                return t.rearrange("p t e -> p (t e)")

            def route(st):
                q = st.slot("R", 2)
                issued = [0]

                def after():
                    dve.wait_ge(rt, st.before("R", RT, issued[0]))

                def done(ins):
                    issued[0] += 1
                    ins.then_inc(rt, 1)

                dve.wait_ge(enx_ready, st.before("R", 1, 1))
                done(v.tensor_scalar(den[:, :], enx[:, :], 1.0, None, ALU.add))
                after()
                done(v.reciprocal(flat(score[:, :, :]), den[:, :]))
                after()
                done(v.tensor_tensor(biased[:, :, :], score[:, :, :],
                                     bias8[:, :].unsqueeze(1).broadcast_to([P, TG, NE]), ALU.add))
                turn(rt, st.before("R", RT, issued[0]))
                for t in range(TG):
                    done(v.max(top8[:, t], biased[:, t]))
                turn(rt, st.before("R", RT, issued[0]))
                for t in range(TG):
                    done(v.max_index(idx8[:, t], top8[:, t], biased[:, t]))
                after()
                done(v.tensor_copy(idxf[:, :, :], idx8[:, :, 0:2]))
                after()
                for n in range(2):
                    done(v.tensor_tensor(hot[:, n], iota_f[:, :].unsqueeze(1).broadcast_to([P, TG, NE]),
                                         idxf[:, :, n:n + 1].broadcast_to([P, TG, NE]), ALU.is_equal))
                after()
                done(v.tensor_tensor(chosen[:, :, :], hot[:, 0], hot[:, 1], ALU.add))
                after()
                done(v.tensor_tensor(raw[:, :, :], chosen[:, :, :], score[:, :, :], ALU.mult))
                after()
                done(v.tensor_reduce(wsum[:, :], raw[:, :, :], AXX, ALU.add))
                after()
                done(v.tensor_scalar(wsum_eps[:, :], wsum[:, :], EPS_W, None, ALU.add))
                after()
                done(v.reciprocal(winv[:, :], wsum_eps[:, :]))
                after()
                if st.later("R", 2):
                    dve.wait_ge(relu_ready, st.before("R", TG, -TG))
                if st.later("R", 2):
                    dve.wait_ge(cwT_done, st.before("R", 1, -1))
                v.tensor_tensor(cw[:, q], raw[:, :, :], winv[:, :].unsqueeze(2).broadcast_to([P, TG, NE]),
                                ALU.mult).then_inc(cw_ready, 1)
                dve.wait_ge(cw_ready, st.before("R", 1, 1))
                done(v.tensor_tensor(coef[:, q], cw[:, q, :, EM], cw[:, q, :, EM + 2], ALU.add))
                assert issued[0] == RT

            def x2T_low(st, c):
                q = st.slot("R", 2)
                dve.wait_ge(x2Thi_ready, st.before("R", HC, c + 1))
                v.tensor_tensor(x2T_lo[:, q, c], ps_sh[c][:, :], x2T_hi[:, q, c].bitcast(F32), ALU.subtract)\
                    .then_inc(x2Tlo_ready, 1)

            def split_weights():
                dve.wait_ge(w_loaded, 16 * N_LOADS)
                dve.wait_ge(whi_ready, NSPLIT)
                for hi, lo, full in ((wgu_hi[:, 0].rearrange("p e c i -> p (e c i)"),
                                      wgu_lo[:, 0].rearrange("p e c i -> p (e c i)"),
                                      wg_st.rearrange("p e c i -> p (e c i)")),
                                     (wgu_hi[:, 1].rearrange("p e c i -> p (e c i)"),
                                      wgu_lo[:, 1].rearrange("p e c i -> p (e c i)"),
                                      wu_st.rearrange("p e c i -> p (e c i)")),
                                     (wd_hi[:, :, :], wd_lo[:, :, :], wd_st)):
                    v.tensor_tensor(lo, full, hi.bitcast(F32), ALU.subtract).then_inc(wlo_ready, 1)

            dve.wait_ge(iota_ready, 1)
            v.tensor_copy(iota_f[:, :], iota_u[:, :]).then_inc(iotaf_ready, 1)
            dve.wait_ge(iotaf_ready, 1)

            def output(st, h):
                k = st.slot("Y", 4)
                dve.wait_ge(y_done, st.before("Y", 2, h + 1))
                dve.wait_ge(relu_added, st.before("Y", 1, 1))
                two = acc[:, k, 2 * h:2 * h + 2].rearrange("p t n -> p (t n)")
                v.tensor_tensor(two, ps_y[h][:, :], two, ALU.add).then_inc(out_ready, 1)

            def body(st):
                c_on, y_on, r_on, b_on, m_on = st.on("C"), st.on("Y"), st.on("R"), st.on("B"), st.chain()
                if st.peeled and st.r == 0 and st.s == 3:
                    split_weights()
                if c_on:
                    q = st.slot("C", 2)
                    dve.wait_ge(rt, st.before("C", RT, RT))
                    for t in range(TG):
                        a = acc[:, st.slot("C", 4), t]
                        v.scalar_tensor_tensor(a, x2[:, q, t], coef[:, q, t:t + 1], a, ALU.mult, ALU.add)\
                            .then_inc(ident_added, 1)
                if r_on:
                    q = st.slot("R", 2)
                    if st.later("R", 1):
                        dve.wait_ge(x2T_ready, st.before("R", HC))
                    if st.later("R", 2):
                        dve.wait_ge(conv_ready, st.before("R", CT, -CT))
                    if st.first("R"):
                        v.memset(x2T[:, q, :, 0:PAD], 0.0).then_inc(halo_ready, 1)
                    else:
                        v.tensor_copy(x2T[:, q, :, 0:PAD], x2T[:, 1 - q, :, GT:GT + PAD]).then_inc(halo_ready, 1)
                    x2T_low(st, 0)
                if c_on:
                    dve.wait_ge(halo_ready, st.before("C", 1, 1))
                    conv_tap(st, 0)
                if r_on:
                    x2T_low(st, 1)
                if c_on:
                    hidden(st, 0)
                    conv_tap(st, 1)
                if r_on:
                    dve.wait_ge(router_done, st.before("R", 1, 1))
                    v.tensor_copy(logits[:, :], ps_sh[0][:, 0:TG * NE]).then_inc(logits_ready, 1)
                if c_on:
                    hid_low(st, 0)
                if st.on("L"):
                    norm1_stats(st)
                if y_on:
                    output(st, 0)
                    output(st, 1)
                if c_on:
                    dve.wait_ge(relu_ready, st.before("C", TG, TG))
                    k = st.slot("C", 4)
                    v.tensor_tensor(acc[:, k], acc[:, k], x2[:, st.slot("C", 2)], ALU.add).then_inc(relu_added, 1)
                    conv_tap(st, 2)
                if m_on:
                    dve.wait_ge(mhi_out, st.chains(1, 1))
                    v.tensor_tensor(m_lo[:, :, :], ps_sh[1][:, :].rearrange("p (c n) -> p c n", c=HC),
                                    m_hi[:, :, :].bitcast(F32), ALU.subtract).then_inc(mlo_out, 1)
                if c_on:
                    hidden(st, 1)
                if b_on:
                    residual(st, 0)
                    norm2_stats(st, 0)
                    residual(st, 1)
                    norm2_stats(st, 1)
                if c_on:
                    hidden(st, 2)
                if r_on:
                    route(st)
                if c_on:
                    hid_low(st, 2)
                    hidden(st, 3)

            steps(dve, body)

        @block.gpsimd
        def _(pool):
            g = nc.gpsimd
            g.memset(ident[:, :], 0.0).then_inc(zeroed, 1)
            pool.wait_ge(zeroed, 1)
            g.affine_select(out=ident[:, :], in_=ident[:, :], compare_op=ALU.not_equal, fill=1.0, base=0,
                            pattern=[[-1, P]], channel_multiplier=1).then_inc(ident_ready, 1)
            g.iota(iota_u[:, :], pattern=[[1, NE]], base=0, channel_multiplier=0).then_inc(iota_ready, 1)
            g.memset(half_neg[:, :], -0.5).then_inc(const_ready, 1)
            g.memset(inv_e[:, :], math.exp(-1.0)).then_inc(const_ready, 1)
            g.memset(eps_ln[:, :], EPS_LN).then_inc(const_ready, 1)
            g.memset(zero4[:, :], 0.0).then_inc(const_ready, 1)
            pool.wait_ge(const_ready, 4)

            def norm_factors(mv, negm, rstd, shift, aggr, aggr_n, veps, veps_n, rstd_ready, rstd_n, ready):
                pool.wait_ge(aggr, aggr_n)
                g.tensor_tensor(mv[:, :, 1], mv[:, :, 1], eps_ln[:, :], ALU.add).then_inc(veps, 1)
                g.tensor_tensor(negm[:, :], zero4[:, :], mv[:, :, 0], ALU.subtract).then_inc(veps, 1)
                pool.wait_ge(veps, veps_n)
                g.tensor_tensor(rstd[:, :], mv[:, :, 1], half_neg[:, :], ALU.pow).then_inc(rstd_ready, 1)
                pool.wait_ge(rstd_ready, rstd_n)
                g.tensor_tensor(shift[:, :], negm[:, :], rstd[:, :], ALU.mult).then_inc(ready, 1)

            def gate_weight(st, e):
                q = st.slot("C", 2)
                if e == 0:
                    pool.wait_ge(cwb_loaded[q], st.uses("C", 2, 16, 16))
                pool.wait_ge(gate_ready, st.before("C", EM, e + 1))
                g.tensor_tensor(gate[:, e % 2], gate[:, e % 2], cwb[:, q, e], ALU.mult).then_inc(gatew_ready, 1)

            def hid_low(st, e):
                pool.wait_ge(hidhi_ready, st.before("C", EM, e + 1))
                g.tensor_tensor(hid_lo[:, 1], hid[:, 1], hid_hi[:, 1].bitcast(F32), ALU.subtract)\
                    .then_inc(hidlo_ready[1], 1)

            def body(st):
                c_on, r_on = st.on("C"), st.on("R")
                if c_on:
                    gate_weight(st, 0)
                if r_on:
                    pool.wait_ge(logits_ready, st.before("R", 1, 1))
                    g.tensor_tensor(enx[:, :], inv_e[:, :], logits[:, :], ALU.pow).then_inc(enx_ready, 1)
                if c_on:
                    gate_weight(st, 1)
                    gate_weight(st, 2)
                    hid_low(st, 1)
                if st.on("L"):
                    if st.later("L", 1):
                        pool.wait_ge(xn_ready, st.before("L", TG))
                    norm_factors(mv1, negm1, rstd1, shift1, aggr1, st.before("L", TG, TG), veps1,
                                 st.before("L", 2, 2), rstd1_ready, st.before("L", 1, 1), shift1_ready)
                if st.on("B"):
                    if st.later("B", 1):
                        pool.wait_ge(x2_ready, st.before("B", TG))
                    norm_factors(mv2, negm2, rstd2, shift2, aggr2, st.before("B", TG, TG), veps2,
                                 st.before("B", 2, 2), rstd2_ready, st.before("B", 1, 1), shift2_ready)
                if c_on:
                    gate_weight(st, 3)
                if st.on("L"):
                    pool.wait_ge(xnhi_ready, st.before("L", 1, 1))
                    g.tensor_tensor(xn_lo[:, st.slot("L", 2)], xn[:, :, :], xn_hi[:, st.slot("L", 2)].bitcast(F32),
                                    ALU.subtract).then_inc(xnlo_ready, 1)
                if c_on:
                    hid_low(st, 3)

            steps(pool, body)


def kernel(**inputs):
    import numpy as np
    import concourse.bacc as bacc
    from concourse.bass_utils import run_bass_kernel_spmd as run

    nc = bacc.Bacc("TRN2", target_bir_lowering=False, num_devices=1)
    a = {k.split("_", 1)[1]: np.asarray(v) for k, v in inputs.items()}
    B, N, H = a["attn_x"].shape
    KC = a["ffn_conv_w"].shape[0]
    EM = a["ffn_Wg"].shape[0]
    laid_out = {
        "x": a["attn_x"].reshape(B * N, H),
        "wq": a["attn_wq"],
        "wkT": a["attn_wk"].T,
        "wvT": a["attn_wv"].T,
        "woT": a["attn_wo"].T,
        "wr": a["ffn_Wr"],
        "rbias": a["ffn_router_bias"],
        "wg": a["ffn_Wg"],
        "wu": a["ffn_Wu"],
        "wd": a["ffn_Wd"],
        "convwb": np.concatenate([a["ffn_conv_w"].reshape(KC, H).T, a["ffn_conv_b"].reshape(H, 1)], axis=1),
    }
    arrays, args = {}, []
    for name, v in laid_out.items():
        v = np.ascontiguousarray(v)
        arrays[f"in_{name}"] = v
        args.append(nc.dram_tensor(f"in_{name}", v.shape, mybir.dt.from_np(v.dtype), kind="ExternalInput").ap())
    group = 4 * P
    args.append(nc.dram_tensor("cw_rows", (B * N // group, EM, group), F32, kind="Internal").ap())
    args.append(nc.dram_tensor("out_0", (B * N, H), F32, kind="ExternalOutput").ap())
    program(nc, *args)
    r = run(nc, [arrays], core_ids=[0])
    return r.results[0]["out_0"].reshape(B, N, H)
```

```python
import math
from contextlib import ExitStack

import concourse.bass as bass
from concourse import mybir

F32 = mybir.dt.float32
F32R = mybir.dt.float32r
U32 = mybir.dt.uint32
ALU = mybir.AluOpType
ACT = mybir.ActivationFunctionType
AXX = mybir.AxisListType.X

P = 128
LAG = {"I": -1, "L": 0, "A": 1, "X": 4, "B": 5, "R": 6, "C": 7, "Y": 8}
UNROLL = 4
EPS_LN = 1e-5
EPS_W = 1e-9


class Step:

    def __init__(self, r, s, groups):
        self.r, self.s, self.groups = r, s, groups
        self.peeled = isinstance(r, int)

    def on(self, stage):
        return not self.peeled or 0 <= UNROLL * self.r + self.s - LAG[stage] < self.groups

    def was_on(self, stage):
        return not self.peeled or 0 <= UNROLL * self.r + self.s - 1 - LAG[stage] < self.groups

    def later(self, stage, n):
        return not self.peeled or UNROLL * self.r + self.s - LAG[stage] >= n

    def first(self, stage):
        return (self.s - LAG[stage]) % UNROLL == 0

    def last(self, stage):
        return (self.s - LAG[stage]) % UNROLL == UNROLL - 1

    def group(self, stage):
        return UNROLL * self.r + (self.s - LAG[stage])

    def slot(self, stage, n):
        return (self.s - LAG[stage]) % n

    def before(self, stage, per=1, extra=0):
        n = self.s - LAG[stage]
        if self.peeled:
            return per * min(max(UNROLL * self.r + n, 0), self.groups) + extra
        return self.r * (UNROLL * per) + (n * per + extra)

    def uses(self, stage, n, per=1, extra=0):
        k = (self.s - LAG[stage]) // n
        return self.r * (UNROLL // n * per) + (k * per + extra)

    def chains(self, per=1, extra=0):
        k = (self.s - LAG["B"] - 1) // UNROLL + 1
        if self.peeled:
            return per * min(max(self.r + k, 0), self.groups // UNROLL) + extra
        return self.r * per + (k * per + extra)

    def chain(self):
        return self.first("B") and self.on("B")


GU_BANK = [k % 3 for k in range(8)]


def program(nc, x, wq, wkT, wvT, woT, wr, rbias, wg, wu, wd, convwb, cw_rows, out):
    T, H = x.shape
    D = wq.shape[0]
    NE = wr.shape[1]
    EM, _, I = wg.shape
    KC = convwb.shape[1] - 1
    HC = H // P
    TG = 4
    GT = TG * P
    NG = T // GT
    SCALE = math.sqrt(3.0 / D)
    assert D == 64 and I == P and HC == 2 and NG % UNROLL == 0
    ROUNDS = (NG + max(LAG.values())) // UNROLL
    LOOP = (LAG["Y"] // UNROLL, NG // UNROLL)

    x_rows = x.rearrange("(n p) f -> p n f", p=P)
    out_rows = out.rearrange("(n p) f -> p n f", p=P)

    ctx = ExitStack()
    with ctx:
        def sb(name, shape, dt=F32):
            return ctx.enter_context(nc.sbuf_tensor(name, shape, dt))

        def bank(name):
            return ctx.enter_context(nc.psum_tensor(name, [P, 512], F32))

        def sem(name):
            return ctx.enter_context(nc.semaphore(name))

        wq_sb = sb("wq_sb", [D, H])
        wkT_sb = sb("wkT_sb", [P, HC, D])
        wvT_sb = sb("wvT_sb", [P, HC, D])
        woT_sb = sb("woT_sb", [D, H])
        wr_sb = sb("wr_sb", [P, HC, NE])
        wgu_hi = sb("wgu_hi", [P, 2, EM, HC, I], F32R)
        wgu_lo = sb("wgu_lo", [P, 2, EM, HC, I], F32R)
        wd_hi = sb("wd_hi", [P, EM, H], F32R)
        wd_lo = sb("wd_lo", [P, EM, H], F32R)
        conv_w = sb("conv_w", [P, HC, KC + 1])
        bias8 = sb("bias8", [P, NE])
        ident = sb("ident", [P, P])
        iota_u = sb("iota_u", [P, NE], U32)
        iota_f = sb("iota_f", [P, NE])
        eps_ln = sb("eps_ln", [P, TG])
        zero4 = sb("zero4", [P, TG])
        half_neg = sb("half_neg", [P, TG])
        inv_e = sb("inv_e", [P, TG * NE])

        xa = sb("xa", [P, 2, TG, H])
        stats1 = sb("stats1", [P, TG, 6])
        mv1 = sb("mv1", [P, TG, 2])
        negm1 = sb("negm1", [P, TG])
        rstd1 = sb("rstd1", [P, TG])
        shift1 = sb("shift1", [P, TG])
        xn = sb("xn", [P, 2, TG, H])
        xn_hl = sb("xn_hl", [P, 2, 2, TG, H], F32R)
        xn_hi, xn_lo = xn_hl[:, :, 0], xn_hl[:, :, 1]
        xnT_hi = sb("xnT_hi", [P, 4, HC, GT], F32R)
        xnT_lo = sb("xnT_lo", [P, 4, HC, GT], F32R)
        gram = sb("gram", [P, 6, P])
        p1 = sb("p1", [P, HC, D])
        et = sb("et", [D, D])
        ff = sb("ff", [D, H])
        m_hi = sb("m_hi", [P, HC, H], F32R)
        m_lo = sb("m_lo", [P, HC, H], F32R)
        acc = sb("acc", [P, 4, TG, H])
        stats2 = sb("stats2", [P, TG, 6])
        mv2 = sb("mv2", [P, TG, 2])
        negm2 = sb("negm2", [P, TG])
        rstd2 = sb("rstd2", [P, TG])
        shift2 = sb("shift2", [P, TG])
        x2 = sb("x2", [P, 2, TG, H])
        PAD = KC - 1
        x2T = sb("x2T", [P, 2, HC, PAD + GT])
        x2T_hi = sb("x2T_hi", [P, 2, HC, GT], F32R)
        x2T_lo = sb("x2T_lo", [P, 2, HC, GT], F32R)
        logits = sb("logits", [P, TG * NE])
        enx = sb("enx", [P, TG * NE])
        den = sb("den", [P, TG * NE])
        score = sb("score", [P, TG, NE])
        biased = sb("biased", [P, TG, NE])
        top8 = sb("top8", [P, TG, 8])
        idx8 = sb("idx8", [P, TG, 8], U32)
        idxf = sb("idxf", [P, TG, 2])
        hot = sb("hot", [P, 2, TG, NE])
        chosen = sb("chosen", [P, TG, NE])
        raw = sb("raw", [P, TG, NE])
        wsum = sb("wsum", [P, TG])
        wsum_eps = sb("wsum_eps", [P, TG])
        winv = sb("winv", [P, TG])
        cw = sb("cw", [P, 2, NE, TG])
        coef = sb("coef", [P, 2, TG])
        cwT = sb("cwT", [EM * TG, P])
        cwb = sb("cwb", [P, 2, EM, GT])
        gate = sb("gate", [P, 2, GT])
        hid = sb("hid", [P, 2, GT])
        hid_hi = sb("hid_hi", [P, 2, GT], F32R)
        hid_lo = sb("hid_lo", [P, 2, GT], F32R)
        conv = sb("conv", [P, HC, GT])
        tick = sb("tick", [1, 1])
        w_stage = cwb[:, :, :, :].rearrange("p a e n -> p (a e n)")
        wg_st = w_stage[:, 0:EM * HC * I].rearrange("p (e c i) -> p e c i", e=EM, c=HC)
        wu_st = w_stage[:, EM * HC * I:2 * EM * HC * I].rearrange("p (e c i) -> p e c i", e=EM, c=HC)
        wd_st = w_stage[:, 2 * EM * HC * I:2 * EM * HC * I + EM * H].rearrange("p (e n) -> p e n", e=EM)

        ps_gram = bank("ps_gram")
        ps_gu = [bank(f"ps_gu{k}") for k in range(3)]
        ps_y = [bank(f"ps_y{h}") for h in range(2)]
        ps_sh = [bank(f"ps_sh{k}") for k in range(2)]

        w_loaded = sem("w_loaded")
        xa_loaded = [sem(f"xa_loaded{k}") for k in range(2)]
        acc_loaded = [sem(f"acc_loaded{k}") for k in range(4)]
        out_stored = [sem(f"out_stored{k}") for k in range(4)]
        cw_stored = sem("cw_stored")
        cwb_loaded = [sem(f"cwb_loaded{k}") for k in range(2)]
        zeroed = sem("zeroed")
        ident_ready = sem("ident_ready")
        const_ready = sem("const_ready")
        iota_ready = sem("iota_ready")
        iotaf_ready = sem("iotaf_ready")
        whi_ready = sem("whi_ready")
        wlo_ready = sem("wlo_ready")
        stat1 = sem("stat1")
        aggr1 = sem("aggr1")
        veps1 = sem("veps1")
        rstd1_ready = sem("rstd1_ready")
        shift1_ready = sem("shift1_ready")
        xn_ready = sem("xn_ready")
        xnhi_ready = sem("xnhi_ready")
        xnlo_ready = sem("xnlo_ready")
        gram_done = sem("gram_done")
        gram_out = sem("gram_out")
        gramT_done, gramT_out = sem("gramT_done"), sem("gramT_out")
        p1_done, p1_out = sem("p1_done"), sem("p1_out")
        et_done, et_out = sem("et_done"), sem("et_out")
        f_done, f_out = sem("f_done"), sem("f_out")
        m_done, mhi_out, mlo_out = sem("m_done"), sem("mhi_out"), sem("mlo_out")
        xnT_done = sem("xnT_done")
        xnThi_ready = sem("xnThi_ready")
        xnTlo_ready = sem("xnTlo_ready")
        attn_done = sem("attn_done")
        x1_ready = sem("x1_ready")
        stat2 = sem("stat2")
        aggr2 = sem("aggr2")
        veps2 = sem("veps2")
        rstd2_ready = sem("rstd2_ready")
        shift2_ready = sem("shift2_ready")
        x2_ready = sem("x2_ready")
        x2T_done = sem("x2T_done")
        x2T_ready = sem("x2T_ready")
        x2Thi_ready = sem("x2Thi_ready")
        x2Tlo_ready = sem("x2Tlo_ready")
        halo_ready = sem("halo_ready")
        router_done = sem("router_done")
        logits_ready = sem("logits_ready")
        enx_ready = sem("enx_ready")
        rt = sem("rt")
        cw_ready = sem("cw_ready")
        cwT_done = sem("cwT_done")
        cwT_ready = sem("cwT_ready")
        gu_done = sem("gu_done")
        gate_ready = sem("gate_ready")
        gatew_ready = sem("gatew_ready")
        hid_ready = sem("hid_ready")
        hidhi_ready = sem("hidhi_ready")
        hidlo_ready = [sem(f"hidlo_ready{k}") for k in range(2)]
        down_done = sem("down_done")
        tap_ready = sem("tap_ready")
        conv_ready = sem("conv_ready")
        ident_added = sem("ident_added")
        relu_ready = sem("relu_ready")
        relu_added = sem("relu_added")
        conv_moved = sem("conv_moved")
        y_done = sem("y_done")
        out_ready = sem("out_ready")

        CT = HC * PAD
        N_LOADS = 7 + 2 * EM + 1
        EARLY = LAG["C"]
        NSPLIT = 3

        def steps(eng, body, stop=LOOP[1]):
            for r in range(LOOP[0]):
                for s in range(UNROLL):
                    body(Step(r, s, NG))
            with eng.Fori(LOOP[0], stop, 1) as r:
                for s in range(UNROLL):
                    body(Step(r, s, NG))
            for r in range(stop, ROUNDS):
                for s in range(UNROLL):
                    body(Step(r, s, NG))

        block = ctx.enter_context(nc.Block())

        @block.sync
        def _(sp):
            def load_x(st):
                if st.later("I", 2):
                    sp.wait_ge(xn_ready, st.before("I", TG, -TG))
                sp.dma_start(xa[:, st.slot("I", 2)], x_rows[:, bass.ds(st.group("I") * TG, TG), :])\
                    .then_inc(xa_loaded[st.slot("I", 2)], 16)

            load_x(Step(0, -1, NG))
            load_x(Step(0, 0, NG))
            sp.dma_start(wq_sb[:, :], wq).then_inc(w_loaded, 16)
            sp.dma_start(wkT_sb[:, :, :], wkT.rearrange("(c p) d -> p c d", p=P)).then_inc(w_loaded, 16)
            sp.dma_start(wvT_sb[:, :, :], wvT.rearrange("(c p) d -> p c d", p=P)).then_inc(w_loaded, 16)
            sp.dma_start(woT_sb[:, :], woT).then_inc(w_loaded, 16)
            sp.dma_start(wr_sb[:, :, :], wr.rearrange("(c p) e -> p c e", p=P)).then_inc(w_loaded, 16)
            sp.dma_start(conv_w[:, :, :], convwb.rearrange("(c p) k -> p c k", p=P)).then_inc(w_loaded, 16)
            sp.dma_start(bias8[:, :], rbias.partition_broadcast(P)).then_inc(w_loaded, 16)
            for e in range(EM):
                sp.dma_start(wg_st[:, e], wg[e].rearrange("(c p) i -> p c i", p=P)).then_inc(w_loaded, 16)
                sp.dma_start(wu_st[:, e], wu[e].rearrange("(c p) i -> p c i", p=P)).then_inc(w_loaded, 16)
            sp.dma_start(wd_st, wd.rearrange("e i n -> i e n")).then_inc(w_loaded, 16)

            def body(st):
                if st.on("I") and not (st.peeled and st.group("I") < 2):
                    load_x(st)
                if st.on("Y"):
                    k = st.slot("Y", 4)
                    for h in range(2):
                        sp.wait_ge(out_ready, st.before("Y", 2, h + 1))
                        sp.dma_start(out_rows[:, bass.ds(st.group("Y") * TG + 2 * h, 2), :],
                                     acc[:, k, 2 * h:2 * h + 2]).then_inc(out_stored[k], 16)
                if st.on("R"):
                    k = st.slot("R", 2)
                    rows = cw_rows[bass.ds(st.group("R"), 1)]
                    sp.wait_ge(cwT_ready, st.before("R", 1, 1))
                    sp.dma_start(rows.rearrange("a e (t n) -> (a e t) n", t=TG), cwT[:, :]).then_inc(cw_stored, 16)
                    sp.wait_ge(cw_stored, st.before("R", 16, 16))
                    if st.peeled and st.before("R") < 2:
                        sp.wait_ge(whi_ready, NSPLIT)
                        sp.wait_ge(wlo_ready, NSPLIT)
                    sp.dma_start(cwb[:, k].rearrange("p e n -> p (e n)"),
                                 rows.rearrange("a e n -> (a e n)").partition_broadcast(P))\
                        .then_inc(cwb_loaded[k], 16)
                if st.on("X"):
                    k = st.slot("X", 4)
                    if st.later("X", 4):
                        sp.wait_ge(out_stored[k], st.uses("X", 4, 32))
                    sp.dma_start(acc[:, k], x_rows[:, bass.ds(st.group("X") * TG, TG), :])\
                        .then_inc(acc_loaded[k], 16)

            steps(sp, body, LOOP[1] - 1)
            for k in range(4):
                sp.wait_ge(out_stored[k], 32 * (NG // 4))
            sp.wait_ge(cw_stored, 16 * NG)

        @block.tensor
        def _(pe):
            def three(dst, a_hi, a_lo, b_hi, b_lo, start, stop):
                nc.tensor.matmul(dst, a_hi, b_hi, start=start, stop=False, skip_group_check=True)
                nc.tensor.matmul(dst, a_hi, b_lo, start=False, stop=False, skip_group_check=True)
                return nc.tensor.matmul(dst, a_lo, b_hi, start=False, stop=stop, skip_group_check=True)

            def gate_up(st, k):
                e, w = divmod(k, 2)
                q = st.slot("C", 2)
                if k == 0:
                    pe.wait_ge(x2Tlo_ready, st.before("C", HC, HC))
                if k >= 3:
                    ke, kw = divmod(k - 3, 2)
                    pe.wait_ge((gate_ready, hid_ready)[kw], st.before("C", EM, ke + 1))
                else:
                    ke, kw = divmod((6, 7, 5)[k], 2)
                    if st.later("C", 1):
                        pe.wait_ge((gate_ready, hid_ready)[kw], st.before("C", EM, ke + 1 - EM))
                for c in range(HC):
                    last = three(ps_gu[GU_BANK[k]][:, :], wgu_hi[:, w, e, c], wgu_lo[:, w, e, c],
                                 x2T_hi[:, q, c], x2T_lo[:, q, c], c == 0, c == HC - 1)
                last.then_inc(gu_done, 1)

            def down(st, stage, e):
                pe.wait_ge(hidlo_ready[e % 2], st.before(stage, EM // 2, e // 2 + 1))
                q = e % 2
                for h in range(2):
                    for k in range(2):
                        tok = slice((2 * h + k) * P, (2 * h + k + 1) * P)
                        last = three(ps_y[h][:, k * H:(k + 1) * H], hid_hi[:, q, tok], hid_lo[:, q, tok],
                                     wd_hi[:, e], wd_lo[:, e], False, e == EM - 1)
                    if h == 0 and e == EM - 1:
                        last.then_inc(y_done, 1)
                last.then_inc(down_done, 1)

            def conv_transpose(st):
                pe.wait_ge(conv_ready, st.before("C", CT, CT))
                if st.later("C", 1):
                    pe.wait_ge(out_ready, st.before("C", 2))
                for h in range(2):
                    for k in range(2):
                        t = 2 * h + k
                        for c in range(HC):
                            at = k * H + c * P
                            last = nc.tensor.matmul(ps_y[h][:, at:at + P], conv[:, c, t * P:(t + 1) * P],
                                                    ident[:, :], is_transpose=True, start=(at == 0), stop=False,
                                                    skip_group_check=True)
                last.then_inc(conv_moved, 1)

            def gram_matrix(st):
                pe.wait_ge(xnlo_ready, st.before("A", 1, 1))
                if st.first("A") and st.chain():
                    pe.wait_ge(mlo_out, st.chains(1, 1))
                q = st.slot("A", 2)
                for t in range(TG):
                    start = st.first("A") and t == 0
                    stop = st.last("A") and t == TG - 1
                    three(ps_gram[:, 0:H], xn_hi[:, q, t, 0:P], xn_lo[:, q, t, 0:P],
                          xn_hi[:, q, t, :], xn_lo[:, q, t, :], start, stop)
                    last = nc.tensor.matmul(ps_gram[:, H:2 * H].rearrange("p (a n) -> p a n", a=2),
                                            xn_hi[:, q, t, P:H], xn_hl[:, q, :, t, P:H],
                                            start=False, stop=stop, skip_group_check=True)
                last.then_inc(gram_done, 1)

            def xn_transpose(st, c):
                pe.wait_ge(xn_ready, st.before("A", TG, TG))
                if c == 1 and st.on("R"):
                    pe.wait_ge(cwT_ready, st.before("R", 1, 1))
                elif st.on("B"):
                    pe.wait_ge(x1_ready, st.before("B", 2, 2 - c))
                elif st.later("A", 1):
                    pe.wait_ge(xnTlo_ready, st.before("A", HC, c - 1))
                for t in range(TG):
                    last = nc.tensor.transpose(ps_sh[c][:, t * P:(t + 1) * P],
                                               xn[:, st.slot("A", 2), t, c * P:(c + 1) * P], ident[:, :])
                last.then_inc(xnT_done, 1)

            def x2_transpose(st, c):
                if st.was_on("A"):
                    pe.wait_ge(xnTlo_ready, st.before("A", HC, c - 1))
                elif c == 0:
                    pe.wait_ge(x1_ready, st.before("B", 2))
                else:
                    pe.wait_ge(cwT_ready, st.before("R"))
                for t in range(TG):
                    if c == 0:
                        pe.wait_ge(x2_ready, st.before("R", TG, t + 1))
                    last = nc.tensor.transpose(ps_sh[c][:, t * P:(t + 1) * P],
                                               x2[:, st.slot("R", 2), t, c * P:(c + 1) * P], ident[:, :])
                last.then_inc(x2T_done, 1)

            def router(st):
                pe.wait_ge(x2T_ready, st.before("R", HC, HC))
                pe.wait_ge(x2Tlo_ready, st.before("R", HC, 1))
                b, q = ps_sh[0], st.slot("R", 2)
                for t in range(TG):
                    for c in range(HC):
                        last = nc.tensor.matmul(b[:, t * NE:(t + 1) * NE],
                                                x2T[:, q, c, PAD + t * P:PAD + (t + 1) * P], wr_sb[:, c],
                                                start=(c == 0), stop=(c == HC - 1))
                last.then_inc(router_done, 1)

            def attention(st, h):
                if h == 0 and st.chain():
                    pe.wait_ge(mlo_out, st.chains(1, 1))
                if h == 0 and st.on("R"):
                    pe.wait_ge(x2Tlo_ready, st.before("R", HC, HC))
                elif h == 0:
                    pe.wait_ge(xnTlo_ready, st.before("A", HC))
                elif st.on("R"):
                    pe.wait_ge(logits_ready, st.before("R", 1, 1))
                else:
                    pe.wait_ge(xnTlo_ready, st.before("A", HC, -1))
                if h == 0:
                    pe.wait_ge(xnTlo_ready, st.before("B", HC, HC))
                b, q = ps_sh[1 - h], st.slot("B", 4)
                for k in range(2):
                    tok = slice((2 * h + k) * P, (2 * h + k + 1) * P)
                    for c in range(HC):
                        last = three(b[:, k * H:(k + 1) * H], xnT_hi[:, q, c, tok], xnT_lo[:, q, c, tok],
                                     m_hi[:, c], m_lo[:, c], c == 0, c == HC - 1)
                last.then_inc(attn_done, 1)

            def weights_transpose(st):
                pe.wait_ge(cw_ready, st.before("R", 1, 1))
                if st.on("B"):
                    pe.wait_ge(x1_ready, st.before("B", 2, 1))
                else:
                    pe.wait_ge(x2Tlo_ready, st.before("R", HC, HC))
                nc.tensor.transpose(ps_sh[1][0:EM * TG, 0:P],
                                    cw[:, st.slot("R", 2), 0:EM].rearrange("p e t -> p (e t)"), ident[:, :])\
                    .then_inc(cwT_done, 1)

            def chain_gramT(st):
                pe.wait_ge(gram_out, st.chains(1, 1))
                nc.tensor.transpose(ps_gram[:, 0:P], gram[:, 1], ident[:, :])
                nc.tensor.transpose(ps_gram[:, P:2 * P], gram[:, 3], ident[:, :]).then_inc(gramT_done, 1)

            def chain_p1(st):
                pe.wait_ge(gramT_out, st.chains(1, 1))
                for m, blocks in enumerate((((0, 0), (4, 1)), ((1, 0), (2, 1), (3, 1), (5, 1)))):
                    for n, (b, c) in enumerate(blocks):
                        last = nc.tensor.matmul(ps_gram[:, m * D:(m + 1) * D], gram[:, b], wvT_sb[:, c],
                                                start=(n == 0), stop=(n == len(blocks) - 1))
                last.then_inc(p1_done, 1)

            def chain_et(st):
                pe.wait_ge(p1_out, st.chains(1, 1))
                for c in range(HC):
                    last = nc.tensor.matmul(ps_gram[0:D, 0:D], p1[:, c], wkT_sb[:, c], start=(c == 0),
                                            stop=(c == HC - 1))
                last.then_inc(et_done, 1)

            def chain_f(st):
                nc.tensor.matmul(ps_gram[0:D, 0:H], et[:, :], woT_sb[:, :], start=True, stop=True).then_inc(f_done, 1)

            def chain_m(st):
                pe.wait_ge(f_out, st.chains(1, 1))
                for c in range(HC):
                    last = nc.tensor.matmul(ps_gram[:, c * H:(c + 1) * H], wq_sb[:, c * P:(c + 1) * P], ff[:, :],
                                            start=True, stop=True)
                last.then_inc(m_done, 1)

            pe.wait_ge(ident_ready, 1)

            def body(st):
                c_on, y_on, r_on, a_on, b_on, m_on = (st.on("C"), st.on("Y"), st.on("R"), st.on("A"), st.on("B"),
                                                      st.chain())
                if st.peeled and b_on and st.before("B") == 0:
                    pe.wait_ge(w_loaded, 16 * N_LOADS)
                if st.peeled and c_on and st.before("C") == 0:
                    pe.wait_ge(wlo_ready, NSPLIT)
                if c_on:
                    gate_up(st, 0)
                    gate_up(st, 1)
                if r_on:
                    x2_transpose(st, 0)
                if y_on:
                    down(st, "Y", EM - 1)
                if m_on:
                    chain_gramT(st)
                if r_on:
                    x2_transpose(st, 1)
                if m_on:
                    chain_p1(st)
                if c_on:
                    gate_up(st, 2)
                if m_on:
                    chain_et(st)
                if r_on:
                    router(st)
                if m_on:
                    pe.wait_ge(et_out, st.chains(1, 1))
                if c_on:
                    gate_up(st, 3)
                if m_on:
                    chain_f(st)
                if c_on:
                    gate_up(st, 4)
                if m_on:
                    chain_m(st)
                if c_on:
                    conv_transpose(st)
                    down(st, "C", 0)
                if b_on and not m_on:
                    attention(st, 0)
                if c_on:
                    gate_up(st, 5)
                if m_on:
                    attention(st, 0)
                if b_on:
                    attention(st, 1)
                if c_on:
                    gate_up(st, 6)
                    down(st, "C", 1)
                    gate_up(st, 7)
                if a_on and not r_on:
                    xn_transpose(st, 0)
                    xn_transpose(st, 1)
                if a_on:
                    gram_matrix(st)
                if r_on:
                    weights_transpose(st)
                if a_on and r_on:
                    xn_transpose(st, 0)
                if c_on:
                    down(st, "C", 2)
                if a_on and r_on:
                    xn_transpose(st, 1)

            steps(pe, body)

        @block.scalar
        def _(act):
            def copy(dst, src, scale=1.0):
                return nc.scalar.activation(dst, src, ACT.Copy, scale=scale)

            def silu(st, e):
                act.wait_ge(gu_done, st.before("C", 2 * EM, 2 * e + 1))
                if st.later("C", 1) or e > 1:
                    act.wait_ge(hid_ready, st.before("C", EM, e - 1))
                nc.scalar.activation(gate[:, e % 2], ps_gu[GU_BANK[2 * e]][:, :], ACT.Silu)\
                    .then_inc(gate_ready, 1)

            def hid_high(st, e):
                act.wait_ge(hid_ready, st.before("C", EM, e + 1))
                if st.later("C", 1) or e > 1:
                    act.wait_ge(down_done, st.before("C", EM, e - 1))
                copy(hid_hi[:, e % 2], hid[:, e % 2]).then_inc(hidhi_ready, 1)

            def x2T_out(st, c):
                act.wait_ge(x2T_done, st.before("R", HC, c + 1))
                q = st.slot("R", 2)
                if c == 0:
                    if st.later("R", 1):
                        act.wait_ge(halo_ready, st.before("R"))
                    if st.later("R", 2):
                        act.wait_ge(conv_ready, st.before("R", CT, -CT))
                        act.wait_ge(gu_done, st.before("R", 2 * EM, -2 * EM))
                copy(x2T[:, q, c, PAD:PAD + GT], ps_sh[c][:, :]).then_inc(x2T_ready, 1)
                copy(x2T_hi[:, q, c], ps_sh[c][:, :]).then_inc(x2Thi_ready, 1)

            def chain_copy(st, done, count, pairs, out_sem, scale=1.0):
                act.wait_ge(done, count)
                for dst, src in pairs:
                    copy(dst, src, scale).then_inc(out_sem, 1)

            def split_weights():
                act.wait_ge(w_loaded, 16 * N_LOADS)
                copy(wgu_hi[:, 0].rearrange("p e c i -> p (e c i)"), wg_st.rearrange("p e c i -> p (e c i)"))\
                    .then_inc(whi_ready, 1)
                copy(wgu_hi[:, 1].rearrange("p e c i -> p (e c i)"), wu_st.rearrange("p e c i -> p (e c i)"))\
                    .then_inc(whi_ready, 1)
                copy(wd_hi[:, :, :], wd_st).then_inc(whi_ready, 1)

            def xnT_high(st, c):
                act.wait_ge(xnT_done, st.before("A", HC, c + 1))
                copy(xnT_hi[:, st.slot("A", 4), c], ps_sh[c][:, :]).then_inc(xnThi_ready, 1)

            def norm1(st):
                q = st.slot("L", 2)
                act.wait_ge(shift1_ready, st.before("L", 1, 1))
                if st.later("L", 2):
                    act.wait_ge(xnlo_ready, st.before("L", 1, -1))
                    act.wait_ge(xnT_done, st.before("L", HC, -HC))
                for t in range(TG):
                    nc.scalar.activation(xn[:, q, t], xa[:, q, t], ACT.Identity, bias=shift1[:, t:t + 1],
                                         scale=rstd1[:, t:t + 1]).then_inc(xn_ready, 1)

            def norm2(st):
                q = st.slot("B", 2)
                act.wait_ge(shift2_ready, st.before("B", 1, 1))
                if st.later("B", 2):
                    act.wait_ge(relu_added, st.before("B", 1, -1))
                    act.wait_ge(x2T_done, st.before("B", HC, -HC))
                for t in range(TG):
                    nc.scalar.activation(x2[:, q, t], acc[:, st.slot("B", 4), t], ACT.Identity,
                                         bias=shift2[:, t:t + 1], scale=rstd2[:, t:t + 1]).then_inc(x2_ready, 1)

            def body(st):
                c_on, r_on, m_on = st.on("C"), st.on("R"), st.chain()
                if st.peeled and st.group("L") == LAG["B"] - 1:
                    split_weights()
                if m_on:
                    chain_copy(st, gram_done, st.before("A"),
                               [(gram[:, 0:4], ps_gram[:, :].rearrange("p (b n) -> p b n", b=4))], gram_out)
                if c_on:
                    silu(st, 0)
                if r_on:
                    x2T_out(st, 0)
                if m_on:
                    chain_copy(st, gramT_done, st.chains(1, 1),
                               [(gram[:, 4:6], ps_gram[:, 0:2 * P].rearrange("p (b n) -> p b n", b=2))], gramT_out)
                if r_on:
                    x2T_out(st, 1)
                if m_on:
                    chain_copy(st, p1_done, st.chains(1, 1),
                               [(p1[:, :, :], ps_gram[:, 0:HC * D].rearrange("p (c d) -> p c d", c=HC))], p1_out)
                if c_on:
                    silu(st, 1)
                if m_on:
                    chain_copy(st, et_done, st.chains(1, 1), [(et[:, :], ps_gram[0:D, 0:D])], et_out)
                if r_on:
                    act.wait_ge(router_done, st.before("R", 1, 1))
                    if st.later("R", 1):
                        act.wait_ge(enx_ready, st.before("R"))
                    copy(logits[:, :], ps_sh[0][:, 0:TG * NE]).then_inc(logits_ready, 1)
                if m_on:
                    chain_copy(st, f_done, st.chains(1, 1), [(ff[:, :], ps_gram[0:D, 0:H])], f_out, SCALE)
                if c_on:
                    hid_high(st, 0)
                if m_on:
                    chain_copy(st, m_done, st.chains(1, 1),
                               [(m_hi[:, :, :], ps_gram[:, :].rearrange("p (c n) -> p c n", c=HC))], mhi_out)
                if c_on:
                    silu(st, 2)
                    q = st.slot("C", 2)
                    for t in range(TG):
                        act.wait_ge(ident_added, st.before("C", TG, t + 1))
                        nc.scalar.activation(x2[:, q, t], x2[:, q, t], ACT.Relu, scale=cw[:, q, EM + 3, t:t + 1])\
                            .then_inc(relu_ready, 1)
                    hid_high(st, 1)
                if r_on:
                    q = st.slot("R", 2)
                    act.wait_ge(x2T_ready, st.before("R", HC, HC))
                    if st.later("R", 1):
                        act.wait_ge(conv_moved, st.before("R"))
                    for c in range(HC):
                        nc.scalar.activation(conv[:, c], x2T[:, q, c, PAD:PAD + GT], ACT.Identity,
                                             bias=conv_w[:, c, KC:KC + 1], scale=conv_w[:, c, PAD:PAD + 1])\
                            .then_inc(tap_ready, 1)
                if c_on:
                    silu(st, 3)
                    hid_high(st, 2)
                if st.on("L"):
                    norm1(st)
                    act.wait_ge(xn_ready, st.before("L", TG, TG))
                    if st.later("L", 2):
                        act.wait_ge(gram_done, st.before("L", 1, -1))
                    copy(xn_hi[:, st.slot("L", 2)], xn[:, st.slot("L", 2)]).then_inc(xnhi_ready, 1)
                if r_on:
                    act.wait_ge(cwT_done, st.before("R", 1, 1))
                    if st.later("R", 1):
                        act.wait_ge(cw_stored, st.before("R", 16))
                    copy(cwT[:, :], ps_sh[1][0:EM * TG, 0:P]).then_inc(cwT_ready, 1)
                if st.on("A") and r_on:
                    xnT_high(st, 0)
                if c_on:
                    hid_high(st, 3)
                if st.on("A") and r_on:
                    xnT_high(st, 1)
                if st.on("B"):
                    norm2(st)

            steps(act, body)

        @block.vector
        def _(dve):
            v = nc.vector

            def turn(sem, count):
                dve.wait_ge(sem, count)
                v.tensor_copy(tick[:, :], iota_f[0:1, 0:1])

            def hidden(st, e):
                dve.wait_ge(gatew_ready, st.before("C", EM, e + 1))
                dve.wait_ge(gu_done, st.before("C", 2 * EM, 2 * e + 2))
                if st.later("C", 1) or e > 1:
                    dve.wait_ge(hidlo_ready[e % 2], st.before("C", EM // 2, e // 2))
                v.tensor_tensor(hid[:, e % 2], ps_gu[GU_BANK[2 * e + 1]][:, :], gate[:, e % 2], ALU.mult)\
                    .then_inc(hid_ready, 1)

            def hid_low(st, e):
                dve.wait_ge(hidhi_ready, st.before("C", EM, e + 1))
                v.tensor_tensor(hid_lo[:, 0], hid[:, 0], hid_hi[:, 0].bitcast(F32), ALU.subtract)\
                    .then_inc(hidlo_ready[0], 1)

            def conv_tap(st, n):
                q, k = st.slot("C", 2), PAD - 1 - n
                for c in range(HC):
                    if n == 0:
                        dve.wait_ge(tap_ready, st.before("C", HC, c + 1))
                    else:
                        dve.wait_ge(conv_ready, st.before("C", CT, HC * (n - 1) + c + 1))
                    v.scalar_tensor_tensor(conv[:, c], x2T[:, q, c, k:k + GT], conv_w[:, c, k:k + 1],
                                           conv[:, c], ALU.mult, ALU.add).then_inc(conv_ready, 1)

            def norm1_stats(st):
                q = st.slot("L", 2)
                dve.wait_ge(xa_loaded[q], st.uses("L", 2, 16, 16))
                if st.later("L", 1):
                    dve.wait_ge(shift1_ready, st.before("L"))
                for t in range(TG):
                    v.bn_stats(stats1[:, t], xa[:, q, t]).then_inc(stat1, 1)
                turn(stat1, st.before("L", TG, TG))
                for t in range(TG):
                    v.bn_aggr(mv1[:, t], stats1[:, t]).then_inc(aggr1, 1)

            def residual(st, h):
                q = st.slot("B", 4)
                dve.wait_ge(attn_done, st.before("B", 2, h + 1))
                if h == 0:
                    dve.wait_ge(acc_loaded[q], st.uses("B", 4, 16, 16))
                two = acc[:, q, 2 * h:2 * h + 2].rearrange("p t n -> p (t n)")
                v.tensor_tensor(two, ps_sh[1 - h][:, :], two, ALU.add).then_inc(x1_ready, 1)

            def norm2_stats(st):
                dve.wait_ge(x1_ready, st.before("B", 2, 2))
                if st.later("B", 1):
                    dve.wait_ge(shift2_ready, st.before("B"))
                for t in range(TG):
                    v.bn_stats(stats2[:, t], acc[:, st.slot("B", 4), t]).then_inc(stat2, 1)
                turn(stat2, st.before("B", TG, TG))
                for t in range(TG):
                    v.bn_aggr(mv2[:, t], stats2[:, t]).then_inc(aggr2, 1)

            RT = 12 + 2 * TG

            def flat(t):
                return t.rearrange("p t e -> p (t e)")

            def route(st):
                q = st.slot("R", 2)
                issued = [0]

                def after():
                    dve.wait_ge(rt, st.before("R", RT, issued[0]))

                def done(ins):
                    issued[0] += 1
                    ins.then_inc(rt, 1)

                dve.wait_ge(enx_ready, st.before("R", 1, 1))
                done(v.tensor_scalar(den[:, :], enx[:, :], 1.0, None, ALU.add))
                after()
                done(v.reciprocal(flat(score[:, :, :]), den[:, :]))
                after()
                done(v.tensor_tensor(biased[:, :, :], score[:, :, :],
                                     bias8[:, :].unsqueeze(1).broadcast_to([P, TG, NE]), ALU.add))
                turn(rt, st.before("R", RT, issued[0]))
                for t in range(TG):
                    done(v.max(top8[:, t], biased[:, t]))
                turn(rt, st.before("R", RT, issued[0]))
                for t in range(TG):
                    done(v.max_index(idx8[:, t], top8[:, t], biased[:, t]))
                after()
                done(v.tensor_copy(idxf[:, :, :], idx8[:, :, 0:2]))
                after()
                for n in range(2):
                    done(v.tensor_tensor(hot[:, n], iota_f[:, :].unsqueeze(1).broadcast_to([P, TG, NE]),
                                         idxf[:, :, n:n + 1].broadcast_to([P, TG, NE]), ALU.is_equal))
                after()
                done(v.tensor_tensor(chosen[:, :, :], hot[:, 0], hot[:, 1], ALU.add))
                after()
                done(v.tensor_tensor(raw[:, :, :], chosen[:, :, :], score[:, :, :], ALU.mult))
                after()
                done(v.tensor_reduce(wsum[:, :], raw[:, :, :], AXX, ALU.add))
                after()
                done(v.tensor_scalar(wsum_eps[:, :], wsum[:, :], EPS_W, None, ALU.add))
                after()
                done(v.reciprocal(winv[:, :], wsum_eps[:, :]))
                after()
                if st.later("R", 2):
                    dve.wait_ge(relu_ready, st.before("R", TG, -TG))
                    dve.wait_ge(cwT_done, st.before("R", 1, -1))
                v.tensor_tensor(cw[:, q].rearrange("p e t -> p t e"), raw[:, :, :],
                                winv[:, :].unsqueeze(2).broadcast_to([P, TG, NE]), ALU.mult).then_inc(cw_ready, 1)
                dve.wait_ge(cw_ready, st.before("R", 1, 1))
                done(v.tensor_tensor(coef[:, q], cw[:, q, EM], cw[:, q, EM + 2], ALU.add))
                assert issued[0] == RT

            def x2T_low(st, c):
                q = st.slot("R", 2)
                dve.wait_ge(x2Thi_ready, st.before("R", HC, c + 1))
                v.tensor_tensor(x2T_lo[:, q, c], ps_sh[c][:, :], x2T_hi[:, q, c].bitcast(F32), ALU.subtract)\
                    .then_inc(x2Tlo_ready, 1)

            def xn_low(st):
                if st.peeled and st.on("A") and st.group("A") < EARLY:
                    q = st.slot("A", 2)
                    dve.wait_ge(xnhi_ready, st.before("A", 1, 1))
                    v.tensor_tensor(xn_lo[:, q], xn[:, q], xn_hi[:, q].bitcast(F32), ALU.subtract)\
                        .then_inc(xnlo_ready, 1)

            def split_weights():
                dve.wait_ge(w_loaded, 16 * N_LOADS)
                dve.wait_ge(whi_ready, NSPLIT)
                for hi, lo, full in ((wgu_hi[:, 0].rearrange("p e c i -> p (e c i)"),
                                      wgu_lo[:, 0].rearrange("p e c i -> p (e c i)"),
                                      wg_st.rearrange("p e c i -> p (e c i)")),
                                     (wgu_hi[:, 1].rearrange("p e c i -> p (e c i)"),
                                      wgu_lo[:, 1].rearrange("p e c i -> p (e c i)"),
                                      wu_st.rearrange("p e c i -> p (e c i)")),
                                     (wd_hi[:, :, :], wd_lo[:, :, :], wd_st)):
                    v.tensor_tensor(lo, full, hi.bitcast(F32), ALU.subtract).then_inc(wlo_ready, 1)

            def output(st, h):
                k = st.slot("Y", 4)
                if h == 0:
                    dve.wait_ge(y_done, st.before("Y", 1, 1))
                else:
                    dve.wait_ge(down_done, st.before("Y", EM, EM))
                dve.wait_ge(relu_added, st.before("Y", 1, 1))
                two = acc[:, k, 2 * h:2 * h + 2].rearrange("p t n -> p (t n)")
                v.tensor_tensor(two, ps_y[h][:, :], two, ALU.add).then_inc(out_ready, 1)

            def body(st):
                c_on, y_on, r_on, b_on, m_on = st.on("C"), st.on("Y"), st.on("R"), st.on("B"), st.chain()
                if st.peeled and st.group("L") == LAG["B"]:
                    split_weights()
                if r_on:
                    xn_low(st)
                    q = st.slot("R", 2)
                    if st.later("R", 1):
                        dve.wait_ge(x2T_ready, st.before("R", HC))
                    if st.later("R", 2):
                        dve.wait_ge(conv_ready, st.before("R", CT, -CT))
                    if st.first("R"):
                        v.memset(x2T[:, q, :, 0:PAD], 0.0).then_inc(halo_ready, 1)
                    else:
                        v.tensor_copy(x2T[:, q, :, 0:PAD], x2T[:, 1 - q, :, GT:GT + PAD]).then_inc(halo_ready, 1)
                if c_on:
                    dve.wait_ge(halo_ready, st.before("C", 1, 1))
                    conv_tap(st, 0)
                if st.on("L"):
                    norm1_stats(st)
                if r_on:
                    x2T_low(st, 0)
                if c_on:
                    conv_tap(st, 1)
                if r_on:
                    x2T_low(st, 1)
                if y_on:
                    output(st, 0)
                    output(st, 1)
                if c_on:
                    hidden(st, 0)
                    conv_tap(st, 2)
                    hid_low(st, 0)
                    hidden(st, 1)
                    q = st.slot("C", 2)
                    dve.wait_ge(rt, st.before("C", RT, RT))
                    for t in range(TG):
                        a = acc[:, st.slot("C", 4), t]
                        v.scalar_tensor_tensor(a, x2[:, q, t], coef[:, q, t:t + 1], a, ALU.mult, ALU.add)\
                            .then_inc(ident_added, 1)
                if m_on:
                    dve.wait_ge(mhi_out, st.chains(1, 1))
                    v.tensor_tensor(m_lo[:, :, :], ps_gram[:, :].rearrange("p (c n) -> p c n", c=HC),
                                    m_hi[:, :, :].bitcast(F32), ALU.subtract).then_inc(mlo_out, 1)
                if c_on:
                    dve.wait_ge(relu_ready, st.before("C", TG, TG))
                    k = st.slot("C", 4)
                    v.tensor_tensor(acc[:, k], acc[:, k], x2[:, st.slot("C", 2)], ALU.add).then_inc(relu_added, 1)
                    hidden(st, 2)
                if r_on and c_on:
                    route(st)
                if c_on:
                    hid_low(st, 2)
                if b_on:
                    residual(st, 0)
                    residual(st, 1)
                    norm2_stats(st)
                if r_on and not c_on:
                    route(st)
                if c_on:
                    hidden(st, 3)
                if st.on("A"):
                    if not r_on:
                        xn_low(st)
                    for c in range(HC):
                        q = st.slot("A", 4)
                        if not r_on:
                            dve.wait_ge(xnT_done, st.before("A", HC, c + 1))
                            v.tensor_copy(xnT_hi[:, q, c], ps_sh[c][:, :]).then_inc(xnThi_ready, 1)
                        dve.wait_ge(xnThi_ready, st.before("A", HC, c + 1))
                        v.tensor_tensor(xnT_lo[:, q, c], ps_sh[c][:, :], xnT_hi[:, q, c].bitcast(F32), ALU.subtract)\
                            .then_inc(xnTlo_ready, 1)

            dve.wait_ge(iota_ready, 1)
            v.tensor_copy(iota_f[:, :], iota_u[:, :]).then_inc(iotaf_ready, 1)
            dve.wait_ge(iotaf_ready, 1)
            steps(dve, body)

        @block.gpsimd
        def _(pool):
            g = nc.gpsimd
            g.memset(ident[:, :], 0.0).then_inc(zeroed, 1)
            pool.wait_ge(zeroed, 1)
            g.affine_select(out=ident[:, :], in_=ident[:, :], compare_op=ALU.not_equal, fill=1.0, base=0,
                            pattern=[[-1, P]], channel_multiplier=1).then_inc(ident_ready, 1)
            g.iota(iota_u[:, :], pattern=[[1, NE]], base=0, channel_multiplier=0).then_inc(iota_ready, 1)
            g.memset(half_neg[:, :], -0.5).then_inc(const_ready, 1)
            g.memset(inv_e[:, :], math.exp(-1.0)).then_inc(const_ready, 1)
            g.memset(eps_ln[:, :], EPS_LN).then_inc(const_ready, 1)
            g.memset(zero4[:, :], 0.0).then_inc(const_ready, 1)
            pool.wait_ge(const_ready, 4)

            def norm_factors(mv, negm, rstd, shift, aggr, aggr_n, veps, veps_n, rstd_ready, rstd_n, ready):
                pool.wait_ge(aggr, aggr_n)
                g.tensor_tensor(mv[:, :, 1], mv[:, :, 1], eps_ln[:, :], ALU.add).then_inc(veps, 1)
                g.tensor_tensor(negm[:, :], zero4[:, :], mv[:, :, 0], ALU.subtract).then_inc(veps, 1)
                pool.wait_ge(veps, veps_n)
                g.tensor_tensor(rstd[:, :], mv[:, :, 1], half_neg[:, :], ALU.pow).then_inc(rstd_ready, 1)
                pool.wait_ge(rstd_ready, rstd_n)
                g.tensor_tensor(shift[:, :], negm[:, :], rstd[:, :], ALU.mult).then_inc(ready, 1)

            def norm1_factors(st):
                if st.on("L"):
                    if st.later("L", 1):
                        pool.wait_ge(xn_ready, st.before("L", TG))
                    norm_factors(mv1, negm1, rstd1, shift1, aggr1, st.before("L", TG, TG), veps1,
                                 st.before("L", 2, 2), rstd1_ready, st.before("L", 1, 1), shift1_ready)

            def gate_weight(st, e):
                q = st.slot("C", 2)
                if e == 0:
                    pool.wait_ge(cwb_loaded[q], st.uses("C", 2, 16, 16))
                pool.wait_ge(gate_ready, st.before("C", EM, e + 1))
                g.tensor_tensor(gate[:, e % 2], gate[:, e % 2], cwb[:, q, e], ALU.mult).then_inc(gatew_ready, 1)

            def hid_low(st, e):
                pool.wait_ge(hidhi_ready, st.before("C", EM, e + 1))
                g.tensor_tensor(hid_lo[:, 1], hid[:, 1], hid_hi[:, 1].bitcast(F32), ALU.subtract)\
                    .then_inc(hidlo_ready[1], 1)

            def body(st):
                c_on, r_on = st.on("C"), st.on("R")
                if not c_on:
                    norm1_factors(st)
                if c_on:
                    gate_weight(st, 0)
                    gate_weight(st, 1)
                if r_on:
                    pool.wait_ge(logits_ready, st.before("R", 1, 1))
                    g.tensor_tensor(enx[:, :], inv_e[:, :], logits[:, :], ALU.pow).then_inc(enx_ready, 1)
                if c_on:
                    gate_weight(st, 2)
                    hid_low(st, 1)
                    norm1_factors(st)
                    gate_weight(st, 3)
                if st.on("B"):
                    if st.later("B", 1):
                        pool.wait_ge(x2_ready, st.before("B", TG))
                    norm_factors(mv2, negm2, rstd2, shift2, aggr2, st.before("B", TG, TG), veps2,
                                 st.before("B", 2, 2), rstd2_ready, st.before("B", 1, 1), shift2_ready)
                if c_on:
                    hid_low(st, 3)
                if st.on("L") and not (st.peeled and st.group("L") < EARLY):
                    if st.peeled and st.group("L") == EARLY:
                        pool.wait_ge(xnlo_ready, EARLY)
                    q = st.slot("L", 2)
                    pool.wait_ge(xnhi_ready, st.before("L", 1, 1))
                    g.tensor_tensor(xn_lo[:, q], xn[:, q], xn_hi[:, q].bitcast(F32), ALU.subtract)\
                        .then_inc(xnlo_ready, 1)

            steps(pool, body)


def kernel(**inputs):
    import numpy as np
    import concourse.bacc as bacc
    from concourse.bass_utils import run_bass_kernel_spmd as run

    nc = bacc.Bacc("TRN2", target_bir_lowering=False, num_devices=1)
    a = {k.split("_", 1)[1]: np.asarray(v) for k, v in inputs.items()}
    B, N, H = a["attn_x"].shape
    KC = a["ffn_conv_w"].shape[0]
    EM = a["ffn_Wg"].shape[0]
    laid_out = {
        "x": a["attn_x"].reshape(B * N, H),
        "wq": a["attn_wq"],
        "wkT": a["attn_wk"].T,
        "wvT": a["attn_wv"].T,
        "woT": a["attn_wo"].T,
        "wr": a["ffn_Wr"],
        "rbias": a["ffn_router_bias"],
        "wg": a["ffn_Wg"],
        "wu": a["ffn_Wu"],
        "wd": a["ffn_Wd"],
        "convwb": np.concatenate([a["ffn_conv_w"].reshape(KC, H).T, a["ffn_conv_b"].reshape(H, 1)], axis=1),
    }
    arrays, args = {}, []
    for name, v in laid_out.items():
        v = np.ascontiguousarray(v)
        arrays[f"in_{name}"] = v
        args.append(nc.dram_tensor(f"in_{name}", v.shape, mybir.dt.from_np(v.dtype), kind="ExternalInput").ap())
    group = 4 * P
    args.append(nc.dram_tensor("cw_rows", (B * N // group, EM, group), F32, kind="Internal").ap())
    args.append(nc.dram_tensor("out_0", (B * N, H), F32, kind="ExternalOutput").ap())
    program(nc, *args)
    r = run(nc, [arrays], core_ids=[0])
    return r.results[0]["out_0"].reshape(B, N, H)
```
